# Optimizing a Trainium2 kernel written in Bass

```python
import numpy as np
import jax
import jax.numpy as jnp

def _softmax(x, axis=-1):
    return jax.nn.softmax(x, axis=axis)

def _gelu(x):
    return jax.nn.gelu(x, approximate=True)

def _silu(x):
    return jax.nn.silu(x)

def _sigmoid(x):
    return jax.nn.sigmoid(x)

def _layernorm(x, axis=-1, eps=1e-05):
    m = jnp.mean(x, axis=axis, keepdims=True)
    v = jnp.var(x, axis=axis, keepdims=True)
    return (x - m) / jnp.sqrt(v + eps)

def _scatter_add(tgt, idx, src, axis=0):
    return tgt.at[idx].add(src)

def _segment_sum(src, seg, n):
    return jax.ops.segment_sum(src, seg, n)
kernel_name = 'mk_seq_postln_d1_jaxref_r8_5084ab'

def setup_inputs(seed: int=0):
    np.random.seed(seed)
    _w = jnp.asarray

    def _L0_attn_setup():
        import jax, jax.numpy as jnp
        import numpy as np
        B, S, H, NH = (2, 256, 128, 16)
        D = H // NH
        FF = 4 * H

        def _layernorm(x, g, b, eps=1e-05):
            mu = jnp.mean(x, axis=-1, keepdims=True)
            var = jnp.mean((x - mu) ** 2, axis=-1, keepdims=True)
            return (x - mu) * jax.lax.rsqrt(var + eps) * g + b

        def _attention(x, wq, bq, wk, bk, wv, bv, wo, bo):
            b, s, _ = x.shape
            q = (x @ wq.T + bq).reshape(b, s, NH, D).transpose(0, 2, 1, 3)
            k = (x @ wk.T + bk).reshape(b, s, NH, D).transpose(0, 2, 1, 3)
            v = (x @ wv.T + bv).reshape(b, s, NH, D).transpose(0, 2, 1, 3)
            scores = jnp.einsum('bhqd,bhkd->bhqk', q, k) / jnp.sqrt(jnp.float32(D))
            causal = jnp.tril(jnp.ones((s, s), jnp.float32))
            att = jax.nn.relu(scores) * causal
            att = att / (jnp.sum(att, axis=-1, keepdims=True) + 1e-09)
            ctx = jnp.einsum('bhqk,bhkd->bhqd', att, v)
            ctx = ctx.transpose(0, 2, 1, 3).reshape(b, s, H)
            return ctx @ wo.T + bo
        key = jax.random.key(seed)
        ks = jax.random.split(key, 20)

        def lin(k, o, i, scale=0.02):
            return jax.random.normal(k, (o, i), jnp.float32) * scale
        inp = {'x': jax.random.normal(ks[0], (B, S, H), jnp.float32), 'sf_w': lin(ks[1], H, H, 0.01), 'sf_b': jnp.zeros((H,), jnp.float32), 'mask': jax.random.bernoulli(ks[2], 0.1, (H, H)).astype(jnp.float32), 'wq': lin(ks[3], H, H), 'bq': jnp.zeros((H,), jnp.float32), 'wk': lin(ks[4], H, H), 'bk': jnp.zeros((H,), jnp.float32), 'wv': lin(ks[5], H, H), 'bv': jnp.zeros((H,), jnp.float32), 'wo': lin(ks[6], H, H), 'bo': jnp.zeros((H,), jnp.float32), 'ff1_w': lin(ks[7], FF, H), 'ff1_b': jnp.zeros((FF,), jnp.float32), 'ff2_w': lin(ks[8], H, FF), 'ff2_b': jnp.zeros((H,), jnp.float32), 'g1': jnp.ones((H,), jnp.float32), 'b1': jnp.zeros((H,), jnp.float32), 'g2': jnp.ones((H,), jnp.float32), 'b2': jnp.zeros((H,), jnp.float32), 'g3': jnp.ones((H,), jnp.float32), 'b3': jnp.zeros((H,), jnp.float32)}
        return inp
    _L0_attn_in = _L0_attn_setup()

    def _L0_ffn_setup():
        import jax, jax.numpy as jnp
        import numpy as np
        DIM = 128
        INTER = 128
        E = 32
        K = 4
        G = 8
        LG = 4
        ROUTE_SCALE = 1.0
        CAP_FACTOR = 1.25
        B, S = (4, 256)

        def _gate(xf, wg):
            logits = xf @ wg.T
            scores = jax.nn.softmax(logits, axis=-1)
            sg = scores.reshape(-1, G, E // G)
            group_scores = sg.max(axis=-1)
            _, gtop = jax.lax.top_k(group_scores, LG)
            keep_g = jnp.sum(jax.nn.one_hot(gtop, G, dtype=jnp.float32), axis=1) > 0
            masked = jnp.where(keep_g[:, :, None], sg, -jnp.inf).reshape(-1, E)
            _, idx = jax.lax.top_k(masked, K)
            w = jnp.take_along_axis(scores, idx, axis=1)
            w = w / (w.sum(-1, keepdims=True) + 1e-09) * ROUTE_SCALE
            return (w.astype(xf.dtype), idx)

        def _forward(x, wg, w1, w2, w3, sw1, sw2, sw3):
            shape = x.shape
            xf = x.reshape(-1, DIM)
            N = xf.shape[0]
            cap = max(1, int(CAP_FACTOR * N * K / E))
            w, idx = _gate(xf, wg)
            fe = idx.reshape(-1)
            oh = jax.nn.one_hot(fe, E, dtype=jnp.int32)
            pos = (jnp.cumsum(oh, axis=0) * oh).sum(-1) - 1
            keep = pos < cap
            dest = jnp.where(keep, fe * cap + pos, E * cap)
            tok = jnp.arange(N * K, dtype=jnp.int32) // K
            buf_tok = jnp.full((E * cap + 1,), N, jnp.int32).at[dest].set(tok)[:-1]
            buf_w = jnp.zeros((E * cap + 1,), x.dtype).at[dest].set(w.reshape(-1))[:-1]
            xp = jnp.concatenate([xf, jnp.zeros((1, DIM), x.dtype)], axis=0)
            xe = xp[buf_tok].reshape(E, cap, DIM)
            h = jax.nn.silu(jnp.einsum('ecd,edh->ech', xe, w1)) * jnp.einsum('ecd,edh->ech', xe, w3)
            out = jnp.einsum('ech,ehd->ecd', h, w2) * buf_w.reshape(E, cap, 1)
            y = jnp.zeros((N + 1, DIM), x.dtype).at[buf_tok].add(out.reshape(E * cap, DIM))[:N]
            z = jax.nn.silu(xf @ sw1) * (xf @ sw3) @ sw2
            return (y + z).reshape(shape)
        key = jax.random.key(seed)
        ks = jax.random.split(key, 9)
        sd = DIM ** (-0.5)
        si = INTER ** (-0.5)
        x = jax.random.normal(ks[0], (B, S, DIM), jnp.float32)
        wg = jax.random.normal(ks[1], (E, DIM), jnp.float32) * sd
        w1 = jax.random.normal(ks[2], (E, DIM, INTER), jnp.float32) * sd
        w3 = jax.random.normal(ks[3], (E, DIM, INTER), jnp.float32) * sd
        w2 = jax.random.normal(ks[4], (E, INTER, DIM), jnp.float32) * si
        sw1 = jax.random.normal(ks[5], (DIM, INTER), jnp.float32) * sd
        sw3 = jax.random.normal(ks[6], (DIM, INTER), jnp.float32) * sd
        sw2 = jax.random.normal(ks[7], (INTER, DIM), jnp.float32) * si
        return dict(x=x, wg=wg, w1=w1, w2=w2, w3=w3, sw1=sw1, sw2=sw2, sw3=sw3)
    _L0_ffn_in = _L0_ffn_setup()
    _d = {'L0_attn_x': _L0_attn_in['x'], 'L0_attn_sf_w': _L0_attn_in['sf_w'], 'L0_attn_sf_b': _L0_attn_in['sf_b'], 'L0_attn_mask': _L0_attn_in['mask'], 'L0_attn_wq': _L0_attn_in['wq'], 'L0_attn_bq': _L0_attn_in['bq'], 'L0_attn_wk': _L0_attn_in['wk'], 'L0_attn_bk': _L0_attn_in['bk'], 'L0_attn_wv': _L0_attn_in['wv'], 'L0_attn_bv': _L0_attn_in['bv'], 'L0_attn_wo': _L0_attn_in['wo'], 'L0_attn_bo': _L0_attn_in['bo'], 'L0_attn_ff1_w': _L0_attn_in['ff1_w'], 'L0_attn_ff1_b': _L0_attn_in['ff1_b'], 'L0_attn_ff2_w': _L0_attn_in['ff2_w'], 'L0_attn_ff2_b': _L0_attn_in['ff2_b'], 'L0_attn_g1': _L0_attn_in['g1'], 'L0_attn_b1': _L0_attn_in['b1'], 'L0_attn_g2': _L0_attn_in['g2'], 'L0_attn_b2': _L0_attn_in['b2'], 'L0_attn_g3': _L0_attn_in['g3'], 'L0_attn_b3': _L0_attn_in['b3'], 'L0_ffn_wg': _L0_ffn_in['wg'], 'L0_ffn_w1': _L0_ffn_in['w1'], 'L0_ffn_w2': _L0_ffn_in['w2'], 'L0_ffn_w3': _L0_ffn_in['w3'], 'L0_ffn_sw1': _L0_ffn_in['sw1'], 'L0_ffn_sw2': _L0_ffn_in['sw2'], 'L0_ffn_sw3': _L0_ffn_in['sw3']}
    _x0 = _d['L0_attn_x']
    _d['L0_attn_x'] = jax.random.normal(jax.random.fold_in(jax.random.key(seed), 1), (16, 512, 128), dtype=_x0.dtype)
    del _x0
    return _d

def reference(L0_attn_x, L0_attn_sf_w, L0_attn_sf_b, L0_attn_mask, L0_attn_wq, L0_attn_bq, L0_attn_wk, L0_attn_bk, L0_attn_wv, L0_attn_bv, L0_attn_wo, L0_attn_bo, L0_attn_ff1_w, L0_attn_ff1_b, L0_attn_ff2_w, L0_attn_ff2_b, L0_attn_g1, L0_attn_b1, L0_attn_g2, L0_attn_b2, L0_attn_g3, L0_attn_b3, L0_ffn_wg, L0_ffn_w1, L0_ffn_w2, L0_ffn_w3, L0_ffn_sw1, L0_ffn_sw2, L0_ffn_sw3):

    def _L0_attn_ref(x, sf_w, sf_b, mask, wq, bq, wk, bk, wv, bv, wo, bo, ff1_w, ff1_b, ff2_w, ff2_b, g1, b1, g2, b2, g3, b3):
        import jax, jax.numpy as jnp
        import numpy as np
        B, S, H, NH = (2, 256, 128, 16)
        D = H // NH
        FF = 4 * H

        def _layernorm(x, g, b, eps=1e-05):
            mu = jnp.mean(x, axis=-1, keepdims=True)
            var = jnp.mean((x - mu) ** 2, axis=-1, keepdims=True)
            return (x - mu) * jax.lax.rsqrt(var + eps) * g + b

        def _attention(x, wq, bq, wk, bk, wv, bv, wo, bo):
            b, s, _ = x.shape
            q = (x @ wq.T + bq).reshape(b, s, NH, D).transpose(0, 2, 1, 3)
            k = (x @ wk.T + bk).reshape(b, s, NH, D).transpose(0, 2, 1, 3)
            v = (x @ wv.T + bv).reshape(b, s, NH, D).transpose(0, 2, 1, 3)
            scores = jnp.einsum('bhqd,bhkd->bhqk', q, k) / jnp.sqrt(jnp.float32(D))
            causal = jnp.tril(jnp.ones((s, s), jnp.float32))
            att = jax.nn.relu(scores) * causal
            att = att / (jnp.sum(att, axis=-1, keepdims=True) + 1e-09)
            ctx = jnp.einsum('bhqk,bhkd->bhqd', att, v)
            ctx = ctx.transpose(0, 2, 1, 3).reshape(b, s, H)
            return ctx @ wo.T + bo
        out = _layernorm(x, g1, b1)
        out = out @ (sf_w * mask).T + sf_b
        x = x + out
        out = _layernorm(x, g2, b2)
        out = _attention(out, wq, bq, wk, bk, wv, bv, wo, bo)
        x = x + out
        out = _layernorm(x, g3, b3)
        out = jax.nn.relu(out @ ff1_w.T + ff1_b)
        out = out @ ff2_w.T + ff2_b
        return x + out

    def _L0_ffn_ref(x, wg, w1, w2, w3, sw1, sw2, sw3):
        import jax, jax.numpy as jnp
        import numpy as np
        DIM = 128
        INTER = 128
        E = 32
        K = 4
        G = 8
        LG = 4
        ROUTE_SCALE = 1.0
        CAP_FACTOR = 1.25
        B, S = (4, 256)

        def _gate(xf, wg):
            logits = xf @ wg.T
            scores = jax.nn.softmax(logits, axis=-1)
            sg = scores.reshape(-1, G, E // G)
            group_scores = sg.max(axis=-1)
            _, gtop = jax.lax.top_k(group_scores, LG)
            keep_g = jnp.sum(jax.nn.one_hot(gtop, G, dtype=jnp.float32), axis=1) > 0
            masked = jnp.where(keep_g[:, :, None], sg, -jnp.inf).reshape(-1, E)
            _, idx = jax.lax.top_k(masked, K)
            w = jnp.take_along_axis(scores, idx, axis=1)
            w = w / (w.sum(-1, keepdims=True) + 1e-09) * ROUTE_SCALE
            return (w.astype(xf.dtype), idx)

        def _forward(x, wg, w1, w2, w3, sw1, sw2, sw3):
            shape = x.shape
            xf = x.reshape(-1, DIM)
            N = xf.shape[0]
            cap = max(1, int(CAP_FACTOR * N * K / E))
            w, idx = _gate(xf, wg)
            fe = idx.reshape(-1)
            oh = jax.nn.one_hot(fe, E, dtype=jnp.int32)
            pos = (jnp.cumsum(oh, axis=0) * oh).sum(-1) - 1
            keep = pos < cap
            dest = jnp.where(keep, fe * cap + pos, E * cap)
            tok = jnp.arange(N * K, dtype=jnp.int32) // K
            buf_tok = jnp.full((E * cap + 1,), N, jnp.int32).at[dest].set(tok)[:-1]
            buf_w = jnp.zeros((E * cap + 1,), x.dtype).at[dest].set(w.reshape(-1))[:-1]
            xp = jnp.concatenate([xf, jnp.zeros((1, DIM), x.dtype)], axis=0)
            xe = xp[buf_tok].reshape(E, cap, DIM)
            h = jax.nn.silu(jnp.einsum('ecd,edh->ech', xe, w1)) * jnp.einsum('ecd,edh->ech', xe, w3)
            out = jnp.einsum('ech,ehd->ecd', h, w2) * buf_w.reshape(E, cap, 1)
            y = jnp.zeros((N + 1, DIM), x.dtype).at[buf_tok].add(out.reshape(E * cap, DIM))[:N]
            z = jax.nn.silu(xf @ sw1) * (xf @ sw3) @ sw2
            return (y + z).reshape(shape)
        return _forward(x, wg, w1, w2, w3, sw1, sw2, sw3)
    x = L0_attn_x
    x = _layernorm(x + _L0_attn_ref(x, L0_attn_sf_w, L0_attn_sf_b, L0_attn_mask, L0_attn_wq, L0_attn_bq, L0_attn_wk, L0_attn_bk, L0_attn_wv, L0_attn_bv, L0_attn_wo, L0_attn_bo, L0_attn_ff1_w, L0_attn_ff1_b, L0_attn_ff2_w, L0_attn_ff2_b, L0_attn_g1, L0_attn_b1, L0_attn_g2, L0_attn_b2, L0_attn_g3, L0_attn_b3), axis=-1)
    x = _layernorm(x + _L0_ffn_ref(x, L0_ffn_wg, L0_ffn_w1, L0_ffn_w2, L0_ffn_w3, L0_ffn_sw1, L0_ffn_sw2, L0_ffn_sw3), axis=-1)
    return x

_drawn_inputs = setup_inputs


def setup_inputs(seed=0):
    import zlib

    import numpy as np

    out = dict(_drawn_inputs(seed))
    spreads = {'L0_attn_sf_b': (0.0, 0.1),
     'L0_attn_bq': (0.0, 0.687),
     'L0_attn_bk': (0.0, 2.0),
     'L0_attn_bv': (0.0, 0.274),
     'L0_attn_bo': (0.0, 0.1),
     'L0_attn_ff1_b': (0.0, 0.1),
     'L0_attn_ff2_b': (0.0, 0.1),
     'L0_attn_g1': (1.0, 0.6),
     'L0_attn_b1': (0.0, 0.733),
     'L0_attn_g2': (1.0, 0.6),
     'L0_attn_b2': (0.0, 0.564),
     'L0_attn_g3': (1.0, 0.6),
     'L0_attn_b3': (0.0, 0.484)}
    factors = {'L0_attn_wq': 3.85, 'L0_attn_wk': 3.841, 'L0_attn_wv': 2.982}
    for name, (base, spread) in spreads.items():
        noise = np.random.default_rng([zlib.crc32(name.encode()), seed]).standard_normal(out[name].shape)
        drawn = base * np.exp(spread * noise) if base else spread * noise
        out[name] = jnp.asarray(drawn.astype(out[name].dtype))
    for name, factor in factors.items():
        out[name] = (out[name] * factor).astype(out[name].dtype)
    return out
```

```python
from contextlib import ExitStack

import concourse.bass as bass
from concourse import mybir

FP32 = mybir.dt.float32
BF16 = mybir.dt.bfloat16
I32 = mybir.dt.int32
U32 = mybir.dt.uint32
ALU = mybir.AluOpType
ACT = mybir.ActivationFunctionType
AX = mybir.AxisListType.X

P = 128
NB, SEQ, D = 16, 512, 128
TILES = SEQ // P
NH, DH = 16, 8
FFC = 4
NE, TOPK, GROUPS, TOPG = 32, 4, 8, 4
GE = NE // GROUPS
NTOK = NB * SEQ
CAP = int(1.25 * NTOK * TOPK / NE)
CT = CAP // P
W_AT, ID_AT = D, D + NE
ROW = D + NE + 1
SLOTS = 20
PARTS_Q = (0, 1, 2, 0, 1, 0)
PARTS_K = (0, 0, 0, 1, 1, 2)
NS = len(PARTS_Q)
LN_EPS, SUM_EPS = 1e-5, 1e-9
FAR = 65536.0


class Batch:

    def __init__(self, r, k):
        self.r, self.k = r, k
        self.n = 2 * r + k
        self.par = k % 2
        self.half = r + k // 2

    def shift(self, by):
        return Batch(self.r, self.k + by)

    def live(self):
        return not isinstance(self.n, int) or 0 <= self.n < NB


def after(engine, semaphore, value):
    if isinstance(value, int) and value <= 0:
        return
    engine.wait_ge(semaphore, value)


def run_sequences(engine, iteration):
    for b in (-1, 0, 1, 2, 3):
        iteration(Batch(0, b))
    with engine.Fori(2, NB // 2 - 1) as r:
        iteration(Batch(r, 0))
        iteration(Batch(r, 1))
    for b in range(NB - 2, NB + 3):
        iteration(Batch(0, b))


def build(nc, x, sfT, maskT, wqT, wkT, wvT, woT, ff1T, ff2T, sf_b, bq, bk, bv, bo, ff1_b, ff2_b,
          g1, b1, g2, b2, g3, b3, wgT, w1, w2, w3, sw1, sw2, sw3, out):
    x_v = x.rearrange("b (t p) d -> b p t d", p=P)
    out_v = out.rearrange("b (t p) d -> b p t d", p=P)
    slots = nc.dram_tensor("slots", [NE * CAP, ROW], FP32, kind="Internal").ap()
    slots_v = slots.rearrange("(e c p) r -> e p c r", p=P, c=CT)
    ysum = [nc.dram_tensor(f"ysum{i}", [NTOK + CAP, D], FP32, kind="Internal").ap() for i in range(2)]
    ysum_v = [y[0:NTOK, :].rearrange("(b t p) d -> b p t d", p=P, t=TILES) for y in ysum]

    z = nc.dram_tensor("z", [NTOK, D], FP32, kind="Internal").ap()
    z_v = z.rearrange("(b t p) d -> b p t d", p=P, t=TILES)
    xT = nc.dram_tensor("xT", [NB, D, SEQ], FP32, kind="Internal").ap()

    with ExitStack() as ctx:
        place = ctx

        def sb(name, shape, dt=FP32):
            return place.enter_context(nc.sbuf_tensor(name, shape, dt))

        def pair(name, shape, dt=FP32):
            return [sb(f"{name}_{i}", shape, dt) for i in range(2)]

        def sem(name):
            return ctx.enter_context(nc.semaphore(name))

        SFT, MASKT, SFW = sb("SFT", [P, D]), sb("MASKT", [P, D]), sb("SFW", [P, D])
        WQ, WK, WV, WO = sb("WQ", [P, D]), sb("WK", [P, D]), sb("WV", [P, D]), sb("WO", [P, D])
        FF1, FF2 = sb("FF1", [P, FFC * P]), sb("FF2", [P, FFC, D])
        WG = sb("WG", [P, NE])
        SW1, SW2, SW3 = sb("SW1", [P, D]), sb("SW2", [P, D]), sb("SW3", [P, D])
        SFB, BV, BO, FF2B = sb("SFB", [P, D]), sb("BV", [P, D]), sb("BO", [P, D]), sb("FF2B", [P, D])
        BQ, BK, BQS = sb("BQ", [P, 1]), sb("BK", [P, 1]), sb("BQS", [P, 1])
        G1, B1, G2, B2 = sb("G1", [P, 1]), sb("B1", [P, 1]), sb("G2", [P, 1]), sb("B2", [P, 1])
        G3, B3, FF1B = sb("G3", [P, 1]), sb("B3", [P, 1]), sb("FF1B", [P, FFC])
        IDENT = sb("IDENT", [P, P])
        CAUSAL = sb("CAUSAL", [P, 2 * P])
        EARLIER, ALLONE = sb("EARLIER", [P, P], BF16), sb("ALLONE", [P, P], BF16)
        NEGHALF, EPS, ZERO, STEP = (sb(n, [P, TILES]) for n in ("NEGHALF", "EPS", "ZERO", "STEP"))
        IOTA_I = sb("IOTA_I", [P, NE], I32)
        IOTA_E, SLOT0 = sb("IOTA_E", [P, NE]), sb("SLOT0", [P, NE])
        TOK_I, TOK = sb("TOK_I", [P, CT], I32), sb("TOK", [P, CT])
        FILL = sb("FILL", [P, CT, ROW])

        TICK, HOLD, POOL_HOLD = sb("TICK", [P, 1]), sb("HOLD", [P, 1]), sb("POOL_HOLD", [P, TILES])
        HOLDS = pair("HOLDS", [P, 1])
        seq_scope = ExitStack()
        place = seq_scope
        X, X1B, XXB = pair("X", [P, TILES, D]), pair("X1B", [P, TILES, D]), pair("XXB", [P, TILES, D])
        X1 = sb("X1", [P, TILES, D])
        XM = sb("XM", [P, TILES, D])
        XS = sb("XS", [P, TILES, D])
        NORM_C, NORM_D = sb("NORM_C", [P, TILES, D]), sb("NORM_D", [P, TILES, D])
        NORM = [NORM_C, NORM_C, NORM_D]
        NORMT_C, NORMT_D = sb("NORMT_C", [P, SEQ]), sb("NORMT_D", [P, SEQ])
        NORMT = [NORMT_C, NORMT_C, NORMT_D]
        STATS = [sb(f"STATS{i}", [P, TILES, 6]) for i in range(4)]
        MV = [sb(f"MV{i}", [P, TILES, 2]) for i in range(4)]
        VE = [sb(f"VE{i}", [P, TILES]) for i in range(4)]
        RSTD = [sb(f"RSTD{i}", [P, TILES]) for i in range(4)]
        QF, KF = sb("QF", [P, SEQ]), sb("KF", [P, SEQ])
        QP = [sb(f"QP{i}", [P, SEQ], BF16) for i in range(3)]
        KP = [sb(f"KP{i}", [P, SEQ], BF16) for i in range(3)]
        QS, KS = pair("QS", [P, NH, SEQ], BF16), pair("KS", [P, NH, SEQ], BF16)
        VONE = pair("VONE", [P, TILES, NH, DH + 1])
        ATT = pair("ATT", [P, 5, 2, 512])
        OSB = sb("OSB", [P, SEQ])
        DEN, RDEN = sb("DEN", [P, TILES, 4]), sb("RDEN", [P, TILES, 4])
        CTX, CTXT = sb("CTX", [P, TILES, D]), sb("CTXT", [P, SEQ])
        H1 = sb("H1", [P, FFC, SEQ])
        ROWS = pair("ROWS", [P, TILES, ROW])
        X2T = sb("X2T", [P, SEQ])
        LG, ML = sb("LG", [P, TILES, NE]), sb("ML", [P, TILES, NE])
        GM, GM8, GIF = sb("GM", [P, TILES, GROUPS]), sb("GM8", [P, TILES, 8]), sb("GIF", [P, TILES, 8])
        GI, IX = sb("GI", [P, TILES, 8], U32), sb("IX", [P, TILES, 8], U32)
        RMAX, ZSUM, RZ = sb("RMAX", [P, TILES]), sb("ZSUM", [P, TILES]), sb("RZ", [P, TILES])
        EQG, KEEP = sb("EQG", [P, TILES * GROUPS, TOPG]), sb("KEEP", [P, TILES * GROUPS])
        NEGB = sb("NEGB", [P, TILES * GROUPS])
        M8, IXF = sb("M8", [P, TILES, 8]), sb("IXF", [P, TILES, 8])
        EQE = sb("EQE", [P, TILES, NE, TOPK])
        SEL = sb("SEL", [P, TILES + 1, NE], BF16)
        EXS, EX, SW, WM = (sb(n, [P, TILES, NE]) for n in ("EXS", "EX", "SW", "WM"))
        WS, WSE, RWS = sb("WS", [P, TILES]), sb("WSE", [P, TILES]), sb("RWS", [P, TILES])
        POS, PB, OVER, PO, PV = (sb(n, [P, TILES, NE]) for n in ("POS", "PB", "OVER", "PO", "PV"))
        CARRY = sb("CARRY", [P, NE])
        D8 = sb("D8", [P, TILES, 8])
        IDX = pair("IDX", [P, TILES, TOPK], I32)

        SC = ctx.enter_context(nc.psum_tensor("SC", [P, 4, 512], FP32))
        O = ctx.enter_context(nc.psum_tensor("O", [P, 512], FP32))
        LA = ctx.enter_context(nc.psum_tensor("LA", [P, 512], FP32))
        LB = ctx.enter_context(nc.psum_tensor("LB", [P, 512], FP32))
        LC = ctx.enter_context(nc.psum_tensor("LC", [P, 512], FP32))

        const_in, filled = sem("const_in"), sem("filled")
        x_in = [sem("x_in0"), sem("x_in1")]
        stack_in = [sem("stack_in0"), sem("stack_in1")]
        rows_sent = [sem("rows_sent0"), sem("rows_sent1")]
        y_stored = [sem("y_stored0"), sem("y_stored1")]
        xT_saved = sem("xT_saved")
        tok_next = sem("tok_next")
        setup_pool, setup_dve, setup_act = sem("setup_pool"), sem("setup_dve"), sem("setup_act")
        dve_slots = sem("dve_slots")
        (xsf_ready, n1_ready, t1_done, n1T_ready, sf_done, x1_ready, x1b_step, x_used, n2_ready, t2_done,
         n2T_ready, q_done, q01_ready, qr_ready, q2_ready, q3_ready, k_done, k01_ready, kr_ready, k2_ready,
         k3_ready, v_done, v_ready) = (sem(n) for n in (
            "xsf_ready", "n1_ready", "t1_done", "n1T_ready", "sf_done", "x1_ready", "x1b_step", "x_used",
            "n2_ready", "t2_done", "n2T_ready", "q_done", "q01_ready", "qr_ready", "q2_ready", "q3_ready",
            "k_done", "k01_ready", "kr_ready", "k2_ready", "k3_ready", "v_done", "v_ready"))
        aggr_done = [sem(f"aggr_done{i}") for i in range(4)]
        eps_added = [sem(f"eps_added{i}") for i in range(4)]
        rstd_ready = [sem(f"rstd_ready{i}") for i in range(4)]
        sc_ready, relu_act, relu_dve = sem("sc_ready"), sem("relu_act"), sem("relu_dve")
        pv_done, o_saved, ot_done, ctx_ready = sem("pv_done"), sem("o_saved"), sem("ot_done"), sem("ctx_ready")
        (ct_done, ctT_ready, wo_done, xm_ready, xsb_ready, n3_ready, t3_done, n3T_ready, ff2_done,
         xf_ready) = (sem(n) for n in ("ct_done", "ctT_ready", "wo_done", "xm_ready", "xsb_ready", "n3_ready",
                                       "t3_done", "n3T_ready", "ff2_done", "xf_ready"))
        ff1_done, h1_ready = sem("ff1_done"), sem("h1_ready")
        (x2_ready, t4_done, x2T_ready, logits_done, lg_ready, rmax_ready, exs_ready, ex_ready, rz_ready,
         sw_ready, sel_ready, wm_ready, counts_done, pos_ready, carry_ready, rws_ready, row_ready,
         idx_ready) = (sem(n) for n in (
            "x2_ready", "t4_done", "x2T_ready", "logits_done", "lg_ready", "rmax_ready", "exs_ready", "ex_ready",
            "rz_ready", "sw_ready", "sel_ready", "wm_ready", "counts_done", "pos_ready", "carry_ready",
            "rws_ready", "row_ready", "idx_ready"))

        consts = [(SFT[:, :], sfT), (MASKT[:, :], maskT), (WQ[:, :], wqT), (WK[:, :], wkT), (WV[:, :], wvT),
                  (WO[:, :], woT), (FF1[:, :], ff1T), (FF2[:, :, :], ff2T.rearrange("(c f) d -> f c d", f=P)),
                  (WG[:, :], wgT), (SW1[:, :], sw1), (SW2[:, :], sw2), (SW3[:, :], sw3),
                  (SFB[:, :], sf_b.partition_broadcast(P)), (BV[:, :], bv.partition_broadcast(P)),
                  (BO[:, :], bo.partition_broadcast(P)), (FF2B[:, :], ff2_b.partition_broadcast(P)),
                  (BQ[:, :], bq), (BK[:, :], bk), (G1[:, :], g1), (B1[:, :], b1), (G2[:, :], g2),
                  (B2[:, :], b2), (G3[:, :], g3), (B3[:, :], b3), (FF1B[:, :], ff1_b)]
        CONST_IN = 16 * len(consts)
        SETUP_POOL, SETUP_DVE = 15, 13
        WHOLE = NTOK // CAP
        FILLS = NE + WHOLE + 3
        STACKED = 16 * 2 * NS
        SENT = 16 * TILES * TOPK
        seq_block = seq_scope.enter_context(nc.Block())

        @seq_block.sync
        def _(sp):
            for dst, src in consts:
                sp.dma_start(dst, src).then_inc(const_in, 16)
            sp.dma_start(X[0][:, :, :], x_v[0]).then_inc(x_in[0], 16)

            def iteration(b):
                c, e, nxt = b.shift(1), b.shift(-2), b.shift(2)
                if nxt.live():
                    after(sp, x_used, nxt.n - 1)
                    sp.dma_start(X[nxt.par][:, :, :], x_v[bass.ds(nxt.n, 1)].rearrange("o p t d -> (o p) t d")
                                 ).then_inc(x_in[nxt.par], 16)
                if e.live():
                    sp.wait_ge(x2_ready, e.n + 1)
                    sp.dma_start(ysum_v[0][bass.ds(e.n, 1)].rearrange("o p t d -> (o p) t d"),
                                 ROWS[e.par][:, :, 0:D]).then_inc(y_stored[e.par], 16)
                    sp.wait_ge(x2T_ready, e.n + 1)
                    sp.dma_start(xT[bass.ds(e.n, 1)].rearrange("o d t -> (o d) t"), X2T[:, :]).then_inc(xT_saved, 16)
                if c.live():
                    after(sp, sc_ready, SLOTS * (c.n - 1))
                    for stack, parts, order, ready in (
                            (QS, QP, PARTS_Q, (q01_ready, q2_ready, q3_ready)),
                            (KS, KP, PARTS_K, (k01_ready, k2_ready, k3_ready))):
                        for part in range(3):
                            sp.wait_ge(ready[part], c.n + 1)
                            for at in range(NS):
                                if order[at] == part:
                                    sp.dma_start(
                                        stack[c.par][DH * at:DH * (at + 1), :, :],
                                        parts[part][:, :].rearrange_multi_partition(
                                            "(d h) t -> d h t", d=DH).to_physical()
                                    ).then_inc(stack_in[c.par], 16)

            run_sequences(sp, iteration)

        @seq_block.gpsimd
        def _(pool):
            nc.gpsimd.memset(IDENT[:, :], 0.0).then_inc(setup_pool, 1)
            nc.gpsimd.memset(CAUSAL[:, :], 1.0).then_inc(setup_pool, 1)
            nc.gpsimd.memset(EARLIER[:, :], 1.0).then_inc(setup_pool, 1)
            nc.gpsimd.memset(NEGHALF[:, :], -0.5).then_inc(setup_pool, 1)
            nc.gpsimd.memset(EPS[:, :], LN_EPS).then_inc(setup_pool, 1)
            nc.gpsimd.memset(ZERO[:, :], 0.0).then_inc(setup_pool, 1)
            nc.gpsimd.memset(STEP[:, :], float(SEQ)).then_inc(setup_pool, 1)
            nc.gpsimd.iota(IOTA_I[:, :], pattern=[[1, NE]], base=0, channel_multiplier=0).then_inc(setup_pool, 1)
            nc.gpsimd.iota(TOK_I[:, :], pattern=[[P, CT]], base=0, channel_multiplier=1).then_inc(setup_pool, 1)
            pool.wait_ge(setup_pool, 9)
            nc.gpsimd.affine_select(out=IDENT[:, :], in_=IDENT[:, :], compare_op=ALU.not_equal, fill=1.0, base=0,
                                    pattern=[[-1, P]], channel_multiplier=1).then_inc(setup_pool, 1)
            causal2 = CAUSAL[:, :].rearrange("p (a q) -> p a q", a=2)
            nc.gpsimd.affine_select(out=causal2, in_=causal2, compare_op=ALU.is_ge, fill=0.0, base=0,
                                    pattern=[[0, 2], [1, P]], channel_multiplier=-1).then_inc(setup_pool, 1)
            nc.gpsimd.affine_select(out=EARLIER[:, :], in_=EARLIER[:, :], compare_op=ALU.is_gt, fill=0.0, base=0,
                                    pattern=[[1, P]], channel_multiplier=-1).then_inc(setup_pool, 1)
            nc.gpsimd.tensor_copy(IOTA_E[:, :], IOTA_I[:, :]).then_inc(setup_pool, 1)
            nc.gpsimd.tensor_copy(TOK[:, :], TOK_I[:, :]).then_inc(setup_pool, 1)
            pool.wait_ge(setup_pool, 14)
            nc.gpsimd.tensor_scalar(SLOT0[:, :], IOTA_E[:, :], float(CAP), 1.0, ALU.mult, ALU.add
                                    ).then_inc(setup_pool, 1)
            pool.wait_ge(const_in, CONST_IN)
            last_slot = pool.to_reg(NE * CAP - 1)

            def rstd(i, b):
                pool.wait_ge(aggr_done[i], b.n + 1)
                nc.gpsimd.tensor_tensor(VE[i][:, :], MV[i][:, :, 1], EPS[:, :], ALU.add).then_inc(eps_added[i], 1)
                pool.wait_ge(eps_added[i], b.n + 1)
                nc.gpsimd.tensor_tensor(RSTD[i][:, :], VE[i][:, :], NEGHALF[:, :], ALU.pow
                                        ).then_inc(rstd_ready[i], 1)

            def row_bc(vec):
                return vec[:, :].unsqueeze(1).to_broadcast([P, TILES, D])

            def scatter(f, at):
                tile, k = divmod(at, TOPK)
                if at == 0:
                    pool.wait_ge(idx_ready, f.n + 1)
                    pool.wait_ge(row_ready, 2 * (f.n + 1))
                    nc.gpsimd.tensor_tensor(TOK[:, 0:TILES], TOK[:, 0:TILES], STEP[:, :], ALU.add
                                            ).then_inc(tok_next, 1)
                    if isinstance(f.n, int) and f.n == 0:
                        pool.wait_ge(filled, 16 * FILLS)
                pool.indirect_dma_start(
                    out=slots[:, :], out_offset=bass.IndirectOffsetOnAxis(ap=IDX[f.par][:, tile, k:k + 1], axis=0),
                    in_=ROWS[f.par][:, tile, :], in_offset=None, bounds_check=last_slot, oob_is_err=False,
                ).then_inc(rows_sent[f.par], 16)

            def iteration(b):
                c, d, e, f = b.shift(1), b.shift(-1), b.shift(-2), b.shift(-3)
                for s in range(SLOTS):
                    if c.live():
                        if s == 0:
                            pool.wait_ge(x_in[c.par], 16 * (c.half + 1))
                            after(pool, x_used, c.n)
                            nc.gpsimd.tensor_tensor(X1[:, :, :], X[c.par][:, :, :], row_bc(SFB), ALU.add
                                                    ).then_inc(xsf_ready, 1)
                        if s == 1:
                            rstd(0, c)
                        if s == 8:
                            rstd(1, c)
                        if s == 10:
                            pool.wait_ge(x1_ready, c.n + 1)
                            after(pool, xm_ready, c.n - 1)
                            nc.gpsimd.tensor_tensor(X1B[c.par][:, :, :], X1[:, :, :], row_bc(BO), ALU.add
                                                    ).then_inc(x1b_step, 1)
                            pool.wait_ge(x1b_step, c.n + 1)
                            nc.gpsimd.tensor_tensor(XXB[c.par][:, :, :], X1B[c.par][:, :, :], X[c.par][:, :, :],
                                                    ALU.add).then_inc(x_used, 1)
                        if s == 12:
                            pool.wait_ge(q01_ready, c.n + 1)
                            nc.gpsimd.tensor_tensor(QF[:, :], QF[:, :], QP[0][:, :], ALU.subtract
                                                    ).then_inc(qr_ready, 1)
                        if s == 13:
                            pool.wait_ge(k01_ready, c.n + 1)
                            nc.gpsimd.tensor_tensor(KF[:, :], KF[:, :], KP[0][:, :], ALU.subtract
                                                    ).then_inc(kr_ready, 1)
                            pool.wait_ge(q2_ready, c.n + 1)
                            nc.gpsimd.tensor_tensor(QP[2][:, :], QF[:, :], QP[1][:, :], ALU.subtract
                                                    ).then_inc(q3_ready, 1)
                        if s == 14:
                            pool.wait_ge(k2_ready, c.n + 1)
                            nc.gpsimd.tensor_tensor(KP[2][:, :], KF[:, :], KP[1][:, :], ALU.subtract
                                                    ).then_inc(k3_ready, 1)
                    if d.live():
                        if s == 11:
                            rstd(2, d)
                        if s == 12:
                            pool.wait_ge(xm_ready, d.n + 1)
                            nc.gpsimd.tensor_tensor(XS[:, :, :], XS[:, :, :], row_bc(FF2B), ALU.add
                                                    ).then_inc(xsb_ready, 1)
                    if e.live():
                        if s == 1:
                            rstd(3, e)
                        if s == 7:
                            pool.wait_ge(rmax_ready, e.n + 1)
                            nc.gpsimd.tensor_tensor(EXS[:, :, :], LG[:, :, :],
                                                    RMAX[:, :].unsqueeze(2).to_broadcast([P, TILES, NE]),
                                                    ALU.subtract).then_inc(exs_ready, 1)
                        if s == 11:
                            pool.wait_ge(rz_ready, e.n + 1)
                            nc.gpsimd.tensor_tensor(SW[:, :, :], EX[:, :, :],
                                                    RZ[:, :].unsqueeze(2).to_broadcast([P, TILES, NE]),
                                                    ALU.mult).then_inc(sw_ready, 1)
                        if s == 19:
                            pool.wait_ge(sel_ready, e.n + 1)
                            pool.wait_ge(sw_ready, e.n + 1)
                            nc.gpsimd.tensor_tensor(WM[:, :, :], SW[:, :, :], SEL[:, 0:TILES, :], ALU.mult
                                                    ).then_inc(wm_ready, 1)
                    if f.live():
                        if s == 3:
                            pool.wait_ge(rws_ready, f.n + 1)
                            nc.gpsimd.tensor_tensor(ROWS[f.par][:, :, W_AT:W_AT + NE], WM[:, :, :],
                                                    RWS[:, :].unsqueeze(2).to_broadcast([P, TILES, NE]),
                                                    ALU.mult).then_inc(row_ready, 1)
                            after(pool, tok_next, f.n)
                            nc.gpsimd.tensor_tensor(ROWS[f.par][:, :, ID_AT], TOK[:, 0:TILES], ZERO[:, :], ALU.add
                                                    ).then_inc(row_ready, 1)
                        if s >= 6:
                            first = (s - 6) + min(s - 6, 2)
                            for at in range(first, first + (2 if s < 8 else 1)):
                                scatter(f, at)

            run_sequences(pool, iteration)

        @seq_block.vector
        def _(dve):
            ticks = [0]

            def base(b):
                return (b.n + 1) * SLOTS

            nc.vector.memset(FILL[:, :, :], 0.0).then_inc(setup_dve, 1)
            nc.vector.memset(ALLONE[:, :], 1.0).then_inc(setup_dve, 1)
            nc.vector.memset(SEL[:, :, :], 0.0).then_inc(setup_dve, 1)
            nc.vector.memset(CARRY[:, :], 0.0).then_inc(setup_dve, 1)
            nc.vector.memset(O[:, :], 0.0).then_inc(setup_dve, 1)
            for i in range(2):
                nc.vector.memset(QS[i][:, :, :], 0.0).then_inc(setup_dve, 1)
                nc.vector.memset(KS[i][:, :, :], 0.0).then_inc(setup_dve, 1)
            dve.wait_ge(setup_pool, SETUP_POOL)
            for i in range(2):
                nc.vector.memset(VONE[i][:, :, :, DH:DH + 1], 1.0).then_inc(setup_dve, 1)
            dve.wait_ge(setup_dve, 1)
            nc.vector.tensor_scalar(FILL[:, :, ID_AT], TOK[:, :], float(NTOK), None, ALU.add).then_inc(setup_dve, 1)
            dve.wait_ge(const_in, CONST_IN)
            nc.vector.tensor_tensor(SFW[:, :], SFT[:, :], MASKT[:, :], ALU.mult).then_inc(setup_dve, 1)

            def stats(i, src):
                for t in range(TILES):
                    last = nc.vector.bn_stats(STATS[i][:, t, :], src[:, t, :])
                return last

            def aggregate(i):
                for t in range(TILES):
                    last = nc.vector.bn_aggr(MV[i][:, t, :], STATS[i][:, t, :])
                last.then_inc(aggr_done[i], 1)

            def normalise(i, dst, src, b):
                dve.wait_ge(rstd_ready[i], b.n + 1)
                for t in range(TILES):
                    last = nc.vector.tensor_scalar(dst[:, t, 0:D], src[:, t, :], MV[i][:, t, 0:1],
                                                   RSTD[i][:, t:t + 1], ALU.subtract, ALU.mult)
                return last

            def tiles(psum):
                return psum[:, :].rearrange("p (t d) -> p t d", t=TILES)

            def mask_group(b, s):
                hg, j = divmod(s, 5)
                dve.wait_ge(sc_ready, SLOTS * b.n + s + 1)
                if j == 0:
                    after(dve, pv_done, 4 * b.n + hg - 1)
                src = SC[:, 2 * (s % 2):2 * (s % 2) + 2, :]
                dst = ATT[hg % 2][:, j, :, :]
                if j < 2:
                    src, dst, mask = src[:, :, 0:P], dst[:, :, 0:P], CAUSAL[:, 0:P].unsqueeze(1).to_broadcast([P, 2, P])
                elif j < 4:
                    src, dst = src[:, :, 0:2 * P], dst[:, :, 0:2 * P]
                    mask = CAUSAL[:, :].unsqueeze(1).to_broadcast([P, 2, 2 * P])
                else:
                    src = src.rearrange("p a (h q) -> p (a h) q", h=2)[:, :, 0:P]
                    dst = dst.rearrange("p a (h q) -> p (a h) q", h=2)[:, :, 0:P]
                    mask = CAUSAL[:, 0:P].unsqueeze(1).to_broadcast([P, 4, P])
                nc.vector.scalar_tensor_tensor(out=dst, in0=src, scalar=0.0, in1=mask, op0=ALU.max, op1=ALU.mult
                                               ).then_inc(relu_dve, 1)

            def context(b, hg, step):
                lc = LC[:, :].rearrange("p (t h r) -> p t h r", t=TILES, h=4)
                if step == 0:
                    dve.wait_ge(ot_done, 4 * b.n + hg + 1)
                    return nc.vector.tensor_scalar(DEN[:, :, :], lc[:, :, :, DH], SUM_EPS, None, ALU.add)
                if step == 1:
                    return nc.vector.reciprocal(RDEN[:, :, :], DEN[:, :, :])
                dst = CTX[:, :, 4 * DH * hg:4 * DH * (hg + 1)].rearrange("p t (h c) -> p t h c", h=4)
                if hg == 0:
                    after(dve, ct_done, b.n)
                nc.vector.tensor_tensor(dst, lc[:, :, :, 0:DH],
                                        RDEN[:, :, :].unsqueeze(3).to_broadcast([P, TILES, 4, DH]),
                                        ALU.mult).then_inc(ctx_ready, 1)
                return None

            def iteration(b):
                c, d, e, f = b.shift(1), b.shift(-1), b.shift(-2), b.shift(-3)
                for s in range(SLOTS):
                    if b.live():
                        mask_group(b, s)
                    after(dve, dve_slots, base(b) + s)
                    last = None
                    if c.live():
                        if s == 0:
                            dve.wait_ge(x_in[c.par], 16 * (c.half + 1))
                            last = stats(0, X[c.par])
                        if s == 2:
                            after(dve, t2_done, c.n)
                            normalise(0, NORM[0], X[c.par], c).then_inc(n1_ready, 1)
                            last = None
                        if s == 6:
                            dve.wait_ge(sf_done, c.n + 1)
                            dve.wait_ge(xsf_ready, c.n + 1)
                            nc.vector.tensor_tensor(X1[:, :, :], tiles(LA), X1[:, :, :], ALU.add
                                                           ).then_inc(x1_ready, 1)
                            last = None
                        if s == 7:
                            last = stats(1, X1)
                        if s == 9:
                            dve.wait_ge(t1_done, c.n + 1)
                            normalise(1, NORM[1], X1, c).then_inc(n2_ready, 1)
                            last = None
                        if s == 13:
                            dve.wait_ge(v_done, c.n + 1)
                            after(dve, pv_done, 4 * (c.n - 1))
                            nc.vector.tensor_tensor(
                                VONE[c.par][:, :, :, 0:DH], LA[:, :].rearrange("p (t h c) -> p t h c", t=TILES, h=NH),
                                BV[:, :].rearrange("p (h c) -> p h c", h=NH).unsqueeze(1).to_broadcast(
                                    [P, TILES, NH, DH]), ALU.add).then_inc(v_ready, 1)
                            last = None
                    if d.live():
                        if 4 <= s < 7:
                            last = context(d, 3, s - 4)
                        if s < 2:
                            last = context(d, 2, s + 1)
                        if s == 9:
                            dve.wait_ge(wo_done, d.n + 1)
                            dve.wait_ge(x_used, d.n + 1)
                            nc.vector.tensor_tensor(XM[:, :, :], tiles(LB), X1B[d.par][:, :, :], ALU.add)
                            nc.vector.tensor_tensor(XS[:, :, :], tiles(LB), XXB[d.par][:, :, :], ALU.add
                                                           ).then_inc(xm_ready, 1)
                            last = None
                        if s == 10:
                            last = stats(2, XM)
                        if s == 12:
                            after(dve, t3_done, d.n)
                            normalise(2, NORM[2], XM, d).then_inc(n3_ready, 1)
                            last = None
                        if s == 19:
                            dve.wait_ge(ff2_done, d.n + 1)
                            dve.wait_ge(xsb_ready, d.n + 1)
                            nc.vector.tensor_tensor(XS[:, :, :], tiles(LB), XS[:, :, :], ALU.add
                                                           ).then_inc(xf_ready, 1)
                            last = None
                    if b.live() and s >= 9 and s % 5 != 2 and s % 5 != 3:
                        hg, step = divmod(s - 9, 5)
                        last = context(b, hg, step)
                    if e.live():
                        if s == 0:
                            last = stats(3, XS)
                        if s == 2:
                            after(dve, rows_sent[e.par], SENT * e.half)
                            after(dve, y_stored[e.par], 16 * e.half)
                            normalise(3, ROWS[e.par], XS, e).then_inc(x2_ready, 1)
                            last = None
                        if s == 5:
                            dve.wait_ge(logits_done, e.n + 1)
                            nc.vector.tensor_copy(LG[:, :, :], LA[:, 0:TILES * NE].rearrange(
                                "p (t e) -> p t e", t=TILES)).then_inc(lg_ready, 1)
                            last = None
                        if s == 6:
                            nc.vector.tensor_reduce(GM[:, :, :], LG[:, :, :].rearrange(
                                "p t (g m) -> p (t g) m", g=GROUPS), AX, ALU.max)
                            after(dve, exs_ready, e.n)
                            nc.vector.tensor_reduce(RMAX[:, :], LG[:, :, :], AX, ALU.max
                                                           ).then_inc(rmax_ready, 1)
                            last = None
                        if s == 7:
                            for t in range(TILES):
                                last = nc.vector.max(GM8[:, t, :], GM[:, t, :])
                        if s == 8:
                            nc.vector.memset(HOLD[:, :], 0.0)
                            for t in range(TILES):
                                last = nc.vector.max_index(GI[:, t, :], GM8[:, t, :], GM[:, t, :])
                        if s == 9:
                            nc.vector.tensor_copy(GIF[:, :, :], GI[:, :, :])
                            dve.wait_ge(ex_ready, e.n + 1)
                            last = nc.vector.tensor_reduce(ZSUM[:, :], EX[:, :, :], AX, ALU.add)
                        if s == 10:
                            nc.vector.tensor_tensor(
                                EQG[:, :, :].rearrange("p (t g) m -> p t g m", t=TILES),
                                GIF[:, :, 0:TOPG].unsqueeze(2).to_broadcast([P, TILES, GROUPS, TOPG]),
                                IOTA_E[:, 0:GROUPS].unsqueeze(1).unsqueeze(3).to_broadcast([P, TILES, GROUPS, TOPG]),
                                ALU.is_equal)
                            after(dve, sw_ready, e.n)
                            nc.vector.reciprocal(RZ[:, :], ZSUM[:, :]).then_inc(rz_ready, 1)
                            last = None
                        if s == 11:
                            last = nc.vector.tensor_reduce(KEEP[:, :], EQG[:, :, :], AX, ALU.max)
                        if s == 12:
                            last = nc.vector.tensor_scalar(NEGB[:, :], KEEP[:, :], 1.0, 1e30, ALU.subtract, ALU.mult)
                        if s == 13:
                            last = nc.vector.tensor_tensor(
                                ML[:, :, :].rearrange("p t (g m) -> p (t g) m", g=GROUPS),
                                LG[:, :, :].rearrange("p t (g m) -> p (t g) m", g=GROUPS),
                                NEGB[:, :].unsqueeze(2).to_broadcast([P, TILES * GROUPS, GE]), ALU.add)
                        if s == 14:
                            for t in range(TILES):
                                last = nc.vector.max(M8[:, t, :], ML[:, t, :])
                        if s == 15:
                            for t in range(TILES):
                                last = nc.vector.max_index(IX[:, t, :], M8[:, t, :], ML[:, t, :])
                        if s == 16:
                            last = nc.vector.tensor_copy(IXF[:, :, :], IX[:, :, :])
                        if s == 17:
                            for t in range(TILES):
                                last = nc.vector.tensor_tensor(
                                    EQE[:, t, :, :],
                                    IXF[:, t, 0:TOPK].unsqueeze(1).to_broadcast([P, NE, TOPK]),
                                    IOTA_E[:, :].unsqueeze(2).to_broadcast([P, NE, TOPK]), ALU.is_equal)
                        if s == 18:
                            after(dve, row_ready, 2 * e.n)
                            after(dve, counts_done, e.n)
                            nc.vector.tensor_reduce(SEL[:, 0:TILES, :], EQE[:, :, :, :], AX, ALU.max
                                                           ).then_inc(sel_ready, 1)
                            last = None
                    if f.live():
                        if s == 0:
                            dve.wait_ge(counts_done, f.n + 1)
                            nc.vector.tensor_tensor(
                                POS[:, :, :], LA[:, 0:TILES * NE].rearrange("p (t e) -> p t e", t=TILES),
                                CARRY[:, :].unsqueeze(1).to_broadcast([P, TILES, NE]), ALU.add)
                            dve.wait_ge(wm_ready, f.n + 1)
                            last = nc.vector.tensor_reduce(WS[:, :], WM[:, :, :], AX, ALU.add)
                        if s == 1:
                            nc.vector.tensor_tensor(CARRY[:, :], CARRY[:, :], LA[:, TILES * NE:(TILES + 1) * NE],
                                                    ALU.add).then_inc(pos_ready, 1)
                            nc.vector.tensor_scalar(WSE[:, :], WS[:, :], SUM_EPS, None, ALU.add)
                            nc.vector.tensor_scalar(OVER[:, :, :], POS[:, :, :], float(CAP), FAR, ALU.is_ge, ALU.mult)
                            last = nc.vector.tensor_tensor(PB[:, :, :], POS[:, :, :],
                                                           SLOT0[:, :].unsqueeze(1).to_broadcast([P, TILES, NE]),
                                                           ALU.add)
                        if s == 2:
                            after(dve, row_ready, 2 * f.n)
                            nc.vector.reciprocal(RWS[:, :], WSE[:, :]).then_inc(rws_ready, 1)
                            last = nc.vector.tensor_tensor(PO[:, :, :], PB[:, :, :], OVER[:, :, :], ALU.add)
                        if s == 3:
                            last = nc.vector.tensor_tensor(PV[:, :, :], PO[:, :, :], SEL[:, 0:TILES, :], ALU.mult)
                        if s == 4:
                            for t in range(TILES):
                                last = nc.vector.max(D8[:, t, :], PV[:, t, :])
                        if s == 5:
                            nc.vector.tensor_scalar(IDX[f.par][:, :, :], D8[:, :, 0:TOPK], 1.0, None,
                                                           ALU.subtract).then_inc(idx_ready, 1)
                            last = None
                    for i, at, batch in ((0, 1, c), (1, 8, c), (2, 11, d), (3, 1, e)):
                        if s == at and batch.live():
                            aggregate(i)
                            last = None
                    if last is None:
                        last = nc.vector.memset(TICK[:, :], 0.0)
                    last.then_inc(dve_slots, 1)

            run_sequences(dve, iteration)

        @seq_block.scalar
        def _(act):
            act.wait_ge(setup_dve, 12)
            for i in range(NE):
                act.dma_start(slots_v[i], FILL[:, :, :]).then_inc(filled, 16)
            for i in range(WHOLE):
                act.dma_start(ysum[1][i * CAP:(i + 1) * CAP, :].rearrange("(c p) d -> p c d", p=P),
                              FILL[:, :, 0:D]).then_inc(filled, 16)
            act.dma_start(ysum[1][WHOLE * CAP:NTOK, :].rearrange("(c p) d -> p c d", p=P),
                          FILL[:, 0:(NTOK - WHOLE * CAP) // P, 0:D]).then_inc(filled, 16)
            for i in range(2):
                act.dma_start(ysum[i][NTOK:NTOK + CAP, :].rearrange("(c p) d -> p c d", p=P),
                              FILL[:, :, 0:D]).then_inc(filled, 16)
            act.wait_ge(const_in, CONST_IN)
            nc.scalar.mul(BQS[:, :], BQ[:, :], DH ** -0.5).then_inc(setup_act, 1)

            def relu_group(b, s):
                hg, j = divmod(s, 5)
                act.wait_ge(relu_dve, SLOTS * b.n + s + 1)
                if j == 0:
                    after(act, pv_done, 4 * b.n + hg - 1)
                src = SC[:, 2 * (s % 2):2 * (s % 2) + 2, :]
                dst = ATT[hg % 2][:, j, :, :]
                if j < 4:
                    lo = P if j < 2 else 2 * P
                    src, dst = src[:, :, lo:512], dst[:, :, lo:512]
                else:
                    src = src.rearrange("p a (h q) -> p (a h) q", h=2)[:, :, P:2 * P]
                    dst = dst.rearrange("p a (h q) -> p (a h) q", h=2)[:, :, P:2 * P]
                nc.scalar.activation(dst, src, ACT.Relu).then_inc(relu_act, 1)

            def save_context(b, hg):
                act.wait_ge(pv_done, 4 * b.n + hg + 1)
                after(act, ot_done, 4 * b.n + hg)
                nc.scalar.copy(OSB[:, :], O[:, :]).then_inc(o_saved, 1)

            def iteration(b):
                c, d, e = b.shift(1), b.shift(-1), b.shift(-2)
                for s in range(SLOTS):
                    if s == 4 and d.live():
                        save_context(d, 3)
                    if s > 4 and s % 5 == 4 and b.live():
                        save_context(b, s // 5 - 1)
                    if b.live():
                        relu_group(b, s)
                    if c.live():
                        if s == 3:
                            act.wait_ge(t1_done, c.n + 1)
                            after(act, v_done, c.n)
                            nc.scalar.activation(NORMT[0][:, :], LA[:, :], ACT.Identity, bias=B1[:, :],
                                                 scale=G1[:, :]).then_inc(n1T_ready, 1)
                        if s == 10:
                            act.wait_ge(t2_done, c.n + 1)
                            act.wait_ge(sf_done, c.n + 1)
                            nc.scalar.activation(NORMT[1][:, :], LA[:, :], ACT.Identity, bias=B2[:, :],
                                                 scale=G2[:, :]).then_inc(n2T_ready, 1)
                        if s == 11:
                            act.wait_ge(q_done, c.n + 1)
                            after(act, q3_ready, c.n)
                            p = c.shift(-1)
                            if p.live():
                                act.wait_ge(stack_in[p.par], STACKED * (p.half + 1))
                            nc.scalar.activation(QF[:, :], LA[:, :], ACT.Identity, bias=BQS[:, :],
                                                 scale=DH ** -0.5)
                            nc.scalar.activation(QP[0][:, :], LA[:, :], ACT.Identity, bias=BQS[:, :],
                                                 scale=DH ** -0.5).then_inc(q01_ready, 1)
                        if s == 12:
                            act.wait_ge(k_done, c.n + 1)
                            after(act, k3_ready, c.n)
                            nc.scalar.activation(KF[:, :], LA[:, :], ACT.Identity, bias=BK[:, :])
                            nc.scalar.activation(KP[0][:, :], LA[:, :], ACT.Identity, bias=BK[:, :]
                                                 ).then_inc(k01_ready, 1)
                            act.wait_ge(qr_ready, c.n + 1)
                            nc.scalar.copy(QP[1][:, :], QF[:, :]).then_inc(q2_ready, 1)
                        if s == 13:
                            act.wait_ge(kr_ready, c.n + 1)
                            nc.scalar.copy(KP[1][:, :], KF[:, :]).then_inc(k2_ready, 1)
                    if d.live():
                        if s == 7:
                            act.wait_ge(ct_done, d.n + 1)
                            after(act, wo_done, d.n)
                            nc.scalar.copy(CTXT[:, :], LB[:, :]).then_inc(ctT_ready, 1)
                        if s == 13:
                            act.wait_ge(t3_done, d.n + 1)
                            after(act, ff1_done, FFC * d.n)
                            nc.scalar.activation(NORMT[2][:, :], LB[:, :], ACT.Identity, bias=B3[:, :],
                                                 scale=G3[:, :]).then_inc(n3T_ready, 1)
                        if 14 <= s < 14 + FFC:
                            i = s - 14
                            act.wait_ge(ff1_done, FFC * d.n + i + 1)
                            if i == 0:
                                after(act, ff2_done, d.n)
                            nc.scalar.activation(H1[:, i, :], LB[:, :], ACT.Relu, bias=FF1B[:, i:i + 1]
                                                 ).then_inc(h1_ready, 1)
                    if e.live():
                        if s == 3:
                            act.wait_ge(t4_done, e.n + 1)
                            after(act, logits_done, e.n)
                            after(act, xT_saved, 16 * e.n)
                            nc.scalar.copy(X2T[:, :], LB[:, :]).then_inc(x2T_ready, 1)
                        if s == 8:
                            act.wait_ge(exs_ready, e.n + 1)
                            after(act, sw_ready, e.n)
                            nc.scalar.activation(EX[:, :, :], EXS[:, :, :], ACT.Exp).then_inc(ex_ready, 1)

            run_sequences(act, iteration)

        @seq_block.tensor
        def _(pe):
            pe.wait_ge(setup_dve, SETUP_DVE)
            pe.wait_ge(setup_pool, SETUP_POOL)
            pe.wait_ge(const_in, CONST_IN)

            def transposes(psum, src):
                for t in range(TILES):
                    last = nc.tensor.transpose(psum[:, t * P:(t + 1) * P], src(t), IDENT[:, :])
                return last

            def by_token(psum, srcT, weight, width):
                for t in range(TILES):
                    last = nc.tensor.matmul(psum[:, t * width:(t + 1) * width], srcT[:, t * P:(t + 1) * P],
                                            weight, start=True, stop=True)
                return last

            def scores(b, s):
                hg, j = divmod(s, 5)
                if s == 0:
                    pe.wait_ge(stack_in[b.par], STACKED * (b.half + 1))
                after(pe, relu_act, SLOTS * b.n + s - 1)
                q, k = QS[b.par], KS[b.par]
                bank = 2 * (s % 2)

                def block(head, at, col, key):
                    return nc.tensor.matmul(SC[:, at, col:col + SEQ - key * P], k[:, head, key * P:(key + 1) * P],
                                            q[:, head, key * P:SEQ], start=True, stop=True)

                for i in range(2):
                    head = 4 * hg + 2 * (j % 2) + i
                    if j < 2:
                        last = block(head, bank + i, 0, 0)
                    elif j < 4:
                        block(head, bank + i, 0, 3)
                        last = block(head, bank + i, P, 1)
                    else:
                        block(4 * hg + 2 * i, bank + i, 0, 2)
                        last = block(4 * hg + 2 * i + 1, bank + i, 2 * P, 2)
                last.then_inc(sc_ready, 1)

            def context(b, hg, key):
                if key == 0:
                    pe.wait_ge(relu_act, SLOTS * b.n + 5 * (hg + 1))
                    pe.wait_ge(v_ready, b.n + 1)
                    after(pe, o_saved, 4 * b.n + hg)
                a = ATT[hg % 2]
                for i in range(4):
                    if key == 0:
                        att = a[:, i // 2, i % 2, :]
                    elif key == 1:
                        att = a[:, 2 + i // 2, i % 2, P:512]
                    elif key == 2:
                        att = a[:, 4, i // 2, 2 * P * (i % 2):2 * P * (i % 2 + 1)]
                    else:
                        att = a[:, 2 + i // 2, i % 2, 0:P]
                    last = nc.tensor.matmul(O[32 * i:32 * i + DH + 1, key * P:SEQ], VONE[b.par][:, key, 4 * hg + i, :],
                                            att, start=key == 0, stop=key == 3)
                if key == 3:
                    last.then_inc(pv_done, 1)

            def context_by_token(b, hg):
                pe.wait_ge(o_saved, 4 * b.n + hg + 1)
                after(pe, ctx_ready, 4 * b.n + hg)
                transposes(LC, lambda t: OSB[:, t * P:(t + 1) * P]).then_inc(ot_done, 1)

            def iteration(b):
                c, d, e = b.shift(1), b.shift(-1), b.shift(-2)
                for s in range(SLOTS):
                    if b.live():
                        scores(b, s)
                    if s < 4 and d.live():
                        context(d, 3, s)
                    if s >= 5 and s % 5 < 4 and b.live():
                        context(b, s // 5 - 1, s % 5)
                    if c.live():
                        if s == 3:
                            pe.wait_ge(n1_ready, c.n + 1)
                            after(pe, v_ready, c.n)
                            after(pe, pos_ready, b.shift(-3).n + 1 if b.shift(-3).live() else 0)
                            transposes(LA, lambda t: NORM[0][:, t, :]).then_inc(t1_done, 1)
                        if s == 6:
                            pe.wait_ge(n1T_ready, c.n + 1)
                            after(pe, lg_ready, e.n + 1 if e.live() else 0)
                            by_token(LA, NORMT[0], SFW[:, :], D).then_inc(sf_done, 1)
                        if s == 10:
                            pe.wait_ge(n2_ready, c.n + 1)
                            transposes(LA, lambda t: NORM[1][:, t, :]).then_inc(t2_done, 1)
                        if s == 11:
                            pe.wait_ge(n2T_ready, c.n + 1)
                            nc.tensor.matmul(LA[:, :], WQ[:, :], NORMT[1][:, :], start=True, stop=True
                                             ).then_inc(q_done, 1)
                        if s == 12:
                            pe.wait_ge(q01_ready, c.n + 1)
                            nc.tensor.matmul(LA[:, :], WK[:, :], NORMT[1][:, :], start=True, stop=True
                                             ).then_inc(k_done, 1)
                        if s == 13:
                            pe.wait_ge(k01_ready, c.n + 1)
                            by_token(LA, NORMT[1], WV[:, :], D).then_inc(v_done, 1)
                    if d.live():
                        if s == 4:
                            context_by_token(d, 3)
                        if s == 7:
                            pe.wait_ge(ctx_ready, 4 * (d.n + 1))
                            after(pe, x2T_ready, e.n + 1 if e.live() else 0)
                            transposes(LB, lambda t: CTX[:, t, :]).then_inc(ct_done, 1)
                        if s == 8:
                            pe.wait_ge(ctT_ready, d.n + 1)
                            by_token(LB, CTXT, WO[:, :], D).then_inc(wo_done, 1)
                        if s == 13:
                            pe.wait_ge(n3_ready, d.n + 1)
                            transposes(LB, lambda t: NORM[2][:, t, :]).then_inc(t3_done, 1)
                        if 14 <= s < 14 + FFC:
                            i = s - 14
                            if i == 0:
                                pe.wait_ge(n3T_ready, d.n + 1)
                            else:
                                pe.wait_ge(h1_ready, FFC * d.n + i)
                            nc.tensor.matmul(LB[:, :], FF1[:, i * P:(i + 1) * P], NORMT[2][:, :],
                                             start=True, stop=True).then_inc(ff1_done, 1)
                        if s == 18:
                            pe.wait_ge(h1_ready, FFC * (d.n + 1))
                            for t in range(TILES):
                                for i in range(FFC):
                                    last = nc.tensor.matmul(LB[:, t * P:(t + 1) * P], H1[:, i, t * P:(t + 1) * P],
                                                            FF2[:, i, :], start=i == 0, stop=i == FFC - 1)
                            last.then_inc(ff2_done, 1)
                    if s > 4 and s % 5 == 4 and b.live():
                        context_by_token(b, s // 5 - 1)
                    if e.live():
                        if s == 3:
                            pe.wait_ge(x2_ready, e.n + 1)
                            transposes(LB, lambda t: ROWS[e.par][:, t, 0:D]).then_inc(t4_done, 1)
                        if s == 4:
                            pe.wait_ge(x2T_ready, e.n + 1)
                            if c.live():
                                pe.wait_ge(n1T_ready, c.n + 1)
                            by_token(LA, X2T, WG[:, :], NE).then_inc(logits_done, 1)
                        if s == 19:
                            pe.wait_ge(sel_ready, e.n + 1)
                            if c.live():
                                pe.wait_ge(v_ready, c.n + 1)
                            nc.tensor.matmul(LA[:, 0:(TILES + 1) * NE], EARLIER[:, :],
                                             SEL[:, :, :].rearrange("p t e -> p (t e)"), start=True, stop=False)
                            for t in range(1, TILES + 1):
                                for before in range(t):
                                    last = nc.tensor.matmul(LA[:, t * NE:(t + 1) * NE], ALLONE[:, :],
                                                            SEL[:, before, :], start=False,
                                                            stop=t == TILES and before == t - 1)
                            last.then_inc(counts_done, 1)

            run_sequences(pe, iteration)

        seq_scope.close()

        experts_scope = ExitStack()
        place = experts_scope
        W1, W2, W3 = pair("W1", [P, D]), pair("W2", [P, D]), pair("W3", [P, D])
        LIST = pair("LIST", [P, CT, ROW])
        WCOL = pair("WCOL", [P, CT])
        IDS = pair("IDS", [P, CT], I32)
        XE, SH, HT = pair("XE", [P, SEQ]), pair("SH", [P, SEQ]), pair("HT", [P, SEQ])
        XSH = sb("XSH", [P, SEQ])
        OUTB, ZB = pair("OUTB", [P, CT, D]), sb("ZB", [P, TILES, D])
        list_in = [sem("list_in0"), sem("list_in1")]
        held = sem("held")
        added = [sem("added0"), sem("added1")]
        xsh_in, z_stored, tr_done, xe_ready, h1_done, h_done, silu_done, ht_ready, ffn_done, out_saved, ids_ready = (
            sem(n) for n in ("xsh_in", "z_stored", "tr_done", "xe_ready", "eh1_done", "h_done", "silu_done",
                             "ht_ready", "ffn_done", "out_saved", "ids_ready"))
        PAIRS = NE // 2
        SHARED = 2
        CHUNKS = [(0, 0, 4), (0, 4, 4), (0, 8, 2), (SHARED, 0, 2), (1, 0, 4), (1, 4, 4), (1, 8, 2), (SHARED, 2, 2)]
        NCH = len(CHUNKS)
        OWN = [k for k, ch in enumerate(CHUNKS) if ch[0] != SHARED]
        LISTED, ADDED = 16 * 5, 16 * CT
        T_BANK, H1_BANK = [SC[:, 0, :], SC[:, 1, :]], [SC[:, 2, :], SC[:, 3, :]]
        H3_BANK, OUT_BANK = [LA[:, :], LB[:, :]], [LC[:, :], O[:, :]]
        block = experts_scope.enter_context(nc.Block())

        def run_pairs(engine, pair_of):
            pair_of(0, True, False)
            with engine.Fori(1, PAIRS - 1) as p:
                pair_of(p, False, False)
            pair_of(PAIRS - 1, False, True)

        @block.sync
        def _(sp):
            for i in range(2):
                sp.wait_ge(rows_sent[i], SENT * NB // 2)
                sp.wait_ge(y_stored[i], 16 * NB // 2)
            sp.wait_ge(xT_saved, 16 * NB)

            def store_z(p):
                sp.wait_ge(out_saved, (p + 1) * NCH)
                sp.dma_start(z_v[bass.ds(p, 1)].rearrange("o p t d -> (o p) t d"), ZB[:, :, :]).then_inc(z_stored, 16)

            def pair_of(p, first, last):
                for q in range(2):
                    e = p * 2 + q
                    after(sp, out_saved, (p - 1) * NCH + 4 * q + 3)
                    sp.dma_start(LIST[q][:, :, :], slots_v[bass.ds(e, 1)].rearrange("o p c r -> (o p) c r")
                                 ).then_inc(list_in[q], 16)
                    sp.dma_start(WCOL[q][:, :].unsqueeze(2),
                                 slots_v[bass.ds(e, 1), :, :, bass.ds(e + W_AT, 1)].rearrange(
                                     "o p c r -> (o p) c r"), allow_slow_non_contiguous=True).then_inc(list_in[q], 16)
                    for dst, src in ((W1, w1), (W3, w3), (W2, w2)):
                        sp.dma_start(dst[q][:, :], src[bass.ds(e, 1)].rearrange("o i j -> (o i) j")
                                     ).then_inc(list_in[q], 16)
                if not first:
                    store_z(p - 1)
                sp.dma_start(XSH[:, :], xT[bass.ds(p, 1)].rearrange("o d t -> (o d) t")).then_inc(xsh_in, 16)
                if last:
                    store_z(p)

            run_pairs(sp, pair_of)

        @block.gpsimd
        def _(pool):
            def pair_of(p, first, last):
                for q in range(2):
                    pool.wait_ge(ids_ready, p * 2 + q + 1)
                    if not first:
                        pool.wait_ge(added[q], p * ADDED)
                    for k, (who, tile0, n) in enumerate(CHUNKS):
                        if who != q:
                            continue
                        pool.wait_ge(out_saved, p * NCH + k + 1)
                        after(pool, held, p * len(OWN) + OWN.index(k))
                        nc.gpsimd.tensor_tensor(POOL_HOLD[:, :], ZERO[:, :], ZERO[:, :], ALU.add).then_inc(held, 1)
                        for tile in range(tile0, tile0 + n):
                            pool.indirect_dma_start(
                                out=ysum[q][:, :],
                                out_offset=bass.IndirectOffsetOnAxis(ap=IDS[q][:, tile:tile + 1], axis=0),
                                in_=OUTB[q][:, tile, :], in_offset=None, compute_op=ALU.add,
                            ).then_inc(added[q], 16)

            run_pairs(pool, pair_of)

        @block.scalar
        def _(act):
            def evacuate(p, j):
                act.wait_ge(tr_done, p * len(OWN) + j + 1)
                n = CHUNKS[OWN[j]][2] * P
                back = (p * NCH + OWN[j - 2] + 1) if j >= 2 else (p - 1) * NCH + OWN[j - 2] + 1
                after(act, h_done, back)
                nc.scalar.copy(XE[j % 2][:, 0:n], T_BANK[j % 2][:, 0:n]).then_inc(xe_ready, 1)

            def pair_of(p, first, last):
                if first:
                    evacuate(p, 0)
                for k, (who, tile0, n) in enumerate(CHUNKS):
                    nxt = (k + 1) % NCH
                    if nxt in OWN and not (last and nxt == 0):
                        evacuate(p + (nxt == 0), OWN.index(nxt))
                    act.wait_ge(h_done, p * NCH + k + 1)
                    after(act, ht_ready, p * NCH + k - 1)
                    nc.scalar.activation(SH[k % 2][:, 0:n * P], H1_BANK[k % 2][:, 0:n * P], ACT.Silu
                                         ).then_inc(silu_done, 1)

            run_pairs(act, pair_of)

        @block.vector
        def _(dve):
            def save(p, k):
                who, tile0, n = CHUNKS[k]
                dve.wait_ge(ffn_done, p * NCH + k + 1)
                src = OUT_BANK[k % 2][:, 0:n * P].rearrange("p (t d) -> p t d", d=D)
                if who == SHARED:
                    if tile0 == 0:
                        after(dve, z_stored, p * 16)
                    nc.vector.tensor_copy(ZB[:, tile0:tile0 + n, :], src).then_inc(out_saved, 1)
                else:
                    if tile0 == 0:
                        after(dve, added[who], p * ADDED)
                    nc.vector.tensor_tensor(
                        OUTB[who][:, tile0:tile0 + n, :], src,
                        WCOL[who][:, tile0:tile0 + n].unsqueeze(2).to_broadcast([P, n, D]), ALU.mult
                    ).then_inc(out_saved, 1)

            def pair_of(p, first, last):
                for k, (who, tile0, n) in enumerate(CHUNKS):
                    if who != SHARED and tile0 == 0:
                        dve.wait_ge(list_in[who], (p + 1) * LISTED)
                        after(dve, added[who], p * ADDED)
                        nc.vector.tensor_copy(IDS[who][:, :], LIST[who][:, :, ID_AT]).then_inc(ids_ready, 1)
                    dve.wait_ge(silu_done, p * NCH + k + 1)
                    after(dve, ffn_done, p * NCH + k - 1)
                    nc.vector.tensor_tensor(HT[k % 2][:, 0:n * P], SH[k % 2][:, 0:n * P],
                                            H3_BANK[k % 2][:, 0:n * P], ALU.mult).then_inc(ht_ready, 1)
                    if k > 0:
                        save(p, k - 1)
                    elif not first:
                        save(p - 1, NCH - 1)
                if last:
                    save(p, NCH - 1)

            run_pairs(dve, pair_of)

        @block.tensor
        def _(pe):
            def transpose(p, j):
                who, tile0, n = CHUNKS[OWN[j]]
                if tile0 == 0:
                    pe.wait_ge(list_in[who], (p + 1) * LISTED)
                after(pe, xe_ready, p * len(OWN) + j - 1)
                for t in range(n):
                    last = nc.tensor.transpose(T_BANK[j % 2][:, t * P:(t + 1) * P], LIST[who][:, tile0 + t, 0:D],
                                               IDENT[:, :])
                last.then_inc(tr_done, 1)

            def up(p, k):
                who, tile0, n = CHUNKS[k]
                if who == SHARED:
                    pe.wait_ge(xsh_in, (p + 1) * 16)
                    moving, first_w, third_w = XSH[:, tile0 * P:(tile0 + n) * P], SW1, SW3
                else:
                    j = OWN.index(k)
                    pe.wait_ge(xe_ready, p * len(OWN) + j + 1)
                    moving, first_w, third_w = XE[j % 2][:, 0:n * P], W1[who], W3[who]
                after(pe, ht_ready, p * NCH + k - 1)
                nc.tensor.matmul(H1_BANK[k % 2][:, 0:n * P], first_w[:, :], moving, start=True, stop=True)
                nc.tensor.matmul(H3_BANK[k % 2][:, 0:n * P], third_w[:, :], moving, start=True, stop=True
                                 ).then_inc(h_done, 1)

            def down(p, k):
                who, tile0, n = CHUNKS[k]
                pe.wait_ge(ht_ready, p * NCH + k + 1)
                after(pe, out_saved, p * NCH + k - 1)
                for t in range(n):
                    last = nc.tensor.matmul(OUT_BANK[k % 2][:, t * P:(t + 1) * P], HT[k % 2][:, t * P:(t + 1) * P],
                                            (SW2 if who == SHARED else W2[who])[:, :], start=True, stop=True)
                last.then_inc(ffn_done, 1)

            def pair_of(p, first, last):
                if first:
                    transpose(p, 0)
                for k in range(NCH):
                    nxt = (k + 1) % NCH
                    if nxt in OWN and not (last and nxt == 0):
                        transpose(p + (nxt == 0), OWN.index(nxt))
                    up(p, k)
                    if k > 0:
                        down(p, k - 1)
                    elif not first:
                        down(p - 1, NCH - 1)
                if last:
                    down(p, NCH - 1)

            run_pairs(pe, pair_of)

        experts_scope.close()

        final_scope = ExitStack()
        place = final_scope
        Y0, Y1, Z, RES = pair("Y0", [P, TILES, D]), pair("Y1", [P, TILES, D]), pair("Z", [P, TILES, D]), pair(
            "RES", [P, TILES, D])
        FSTATS, FMV = pair("FSTATS", [P, TILES, 6]), pair("FMV", [P, TILES, 2])
        FVE, FRSTD = pair("FVE", [P, TILES]), pair("FRSTD", [P, TILES])
        y_in = [sem("y_in0"), sem("y_in1")]
        out_stored = [sem("out_stored0"), sem("out_stored1")]
        part_ready, sum_ready, fstats_done, faggr_done, feps_added, frstd_ready, res_ready = (sem(n) for n in (
            "part_ready", "sum_ready", "fstats_done", "faggr_done", "feps_added", "frstd_ready", "res_ready"))
        block = final_scope.enter_context(nc.Block())

        @block.sync
        def _(sp):
            for q in range(2):
                sp.wait_ge(added[q], ADDED * PAIRS)
            sp.wait_ge(z_stored, 16 * PAIRS)

            def load(b):
                after(sp, res_ready, b.n - 1)
                for dst, src in ((Y0, ysum_v[0]), (Y1, ysum_v[1]), (Z, z_v)):
                    sp.dma_start(dst[b.par][:, :, :], src[bass.ds(b.n, 1)].rearrange("o p t d -> (o p) t d")
                                 ).then_inc(y_in[b.par], 16)

            load(Batch(0, 0))
            load(Batch(0, 1))
            with sp.Fori(1, NB // 2) as r:
                load(Batch(r, 0))
                load(Batch(r, 1))

        @block.gpsimd
        def _(pool):
            def both(r):
                for b in (Batch(r, 0), Batch(r, 1)):
                    pool.wait_ge(part_ready, b.n + 1)
                    nc.gpsimd.tensor_tensor(Y0[b.par][:, :, :], Y0[b.par][:, :, :], Z[b.par][:, :, :], ALU.add
                                            ).then_inc(sum_ready, 1)
                for b in (Batch(r, 0), Batch(r, 1)):
                    pool.wait_ge(faggr_done, b.n + 1)
                    nc.gpsimd.tensor_tensor(FVE[b.par][:, :], FMV[b.par][:, :, 1], EPS[:, :], ALU.add
                                            ).then_inc(feps_added, 1)
                for b in (Batch(r, 0), Batch(r, 1)):
                    pool.wait_ge(feps_added, b.n + 1)
                    nc.gpsimd.tensor_tensor(FRSTD[b.par][:, :], FVE[b.par][:, :], NEGHALF[:, :], ALU.pow
                                            ).then_inc(frstd_ready, 1)

            both(0)
            with pool.Fori(1, NB // 2) as r:
                both(r)

        @block.vector
        def _(dve):
            def both(r):
                pair_b = (Batch(r, 0), Batch(r, 1))
                for b in pair_b:
                    dve.wait_ge(y_in[b.par], 48 * (b.half + 1))
                    nc.vector.tensor_tensor(Y0[b.par][:, :, :], Y0[b.par][:, :, :], Y1[b.par][:, :, :], ALU.add
                                            ).then_inc(part_ready, 1)
                for b in pair_b:
                    dve.wait_ge(sum_ready, b.n + 1)
                    for t in range(TILES):
                        last = nc.vector.bn_stats(FSTATS[b.par][:, t, :], Y0[b.par][:, t, :])
                    last.then_inc(fstats_done, 1)
                for b in pair_b:
                    dve.wait_ge(fstats_done, b.n + 1)
                    after(dve, res_ready, b.n - 1)
                    nc.vector.memset(HOLDS[b.par][:, :], 0.0)
                    for t in range(TILES):
                        last = nc.vector.bn_aggr(FMV[b.par][:, t, :], FSTATS[b.par][:, t, :])
                    last.then_inc(faggr_done, 1)
                for b in pair_b:
                    dve.wait_ge(frstd_ready, b.n + 1)
                    after(dve, out_stored[b.par], 16 * b.half)
                    for t in range(TILES):
                        last = nc.vector.tensor_scalar(RES[b.par][:, t, :], Y0[b.par][:, t, :], FMV[b.par][:, t, 0:1],
                                                       FRSTD[b.par][:, t:t + 1], ALU.subtract, ALU.mult)
                    last.then_inc(res_ready, 1)

            both(0)
            with dve.Fori(1, NB // 2) as r:
                both(r)

        @block.scalar
        def _(act):
            def store(b):
                act.wait_ge(res_ready, b.n + 1)
                act.dma_start(out_v[bass.ds(b.n, 1)].rearrange("o p t d -> (o p) t d"), RES[b.par][:, :, :]
                              ).then_inc(out_stored[b.par], 16)

            with act.Fori(0, NB // 2) as r:
                store(Batch(r, 0))
                store(Batch(r, 1))
            for q in range(2):
                act.wait_ge(out_stored[q], 16 * NB // 2)

        final_scope.close()

_INS = ["x", "sfT", "maskT", "wqT", "wkT", "wvT", "woT", "ff1T", "ff2T", "sf_b", "bq", "bk", "bv", "bo", "ff1_b",
        "ff2_b", "g1", "b1", "g2", "b2", "g3", "b3", "wgT", "w1", "w2", "w3", "sw1", "sw2", "sw3"]


def kernel(**inputs):
    import numpy as _np
    import concourse.bacc as _bacc
    from concourse import mybir as _mybir
    from concourse.bass_utils import run_bass_kernel_spmd as _run

    a = {n.split("_", 2)[2]: v for n, v in inputs.items() if n.startswith("L0_attn_")}
    m = {n.split("_", 2)[2]: v for n, v in inputs.items() if n.startswith("L0_ffn_")}

    def by_width(w):
        w = _np.asarray(w)
        return w.reshape(NH, DH, -1).transpose(1, 0, 2).reshape(w.shape[0], -1)

    def col(v):
        return _np.asarray(v).reshape(-1, 1)

    laid = {"x": a["x"], "sfT": a["sf_w"].T, "maskT": a["mask"].T, "wqT": by_width(a["wq"]).T,
            "wkT": by_width(a["wk"]).T, "wvT": a["wv"].T, "woT": a["wo"].T, "ff1T": a["ff1_w"].T,
            "ff2T": a["ff2_w"].T, "sf_b": a["sf_b"], "bq": by_width(a["bq"]), "bk": by_width(a["bk"]),
            "bv": a["bv"], "bo": a["bo"], "ff1_b": a["ff1_b"].reshape(FFC, P).T, "ff2_b": a["ff2_b"],
            "g1": col(a["g1"]), "b1": col(a["b1"]), "g2": col(a["g2"]), "b2": col(a["b2"]),
            "g3": col(a["g3"]), "b3": col(a["b3"]), "wgT": m["wg"].T, "w1": m["w1"], "w2": m["w2"],
            "w3": m["w3"], "sw1": m["sw1"], "sw2": m["sw2"], "sw3": m["sw3"]}

    nc = _bacc.Bacc("TRN2", target_bir_lowering=False, num_devices=1)
    arrays, args = {}, []
    for name in _INS:
        v = _np.ascontiguousarray(laid[name])
        arrays[f"in_{name}_dram"] = v
        args.append(nc.dram_tensor(f"in_{name}_dram", v.shape, _mybir.dt.from_np(v.dtype), kind="ExternalInput").ap())
    args.append(nc.dram_tensor("out_0_dram", (NB, SEQ, D), _mybir.dt.float32, kind="ExternalOutput").ap())
    build(nc, *args)
    r = _run(nc, [arrays], core_ids=[0])
    return r.results[0]["out_0_dram"]
```

```python
from contextlib import ExitStack

import concourse.bass as bass
from concourse import mybir

FP32 = mybir.dt.float32
BF16 = mybir.dt.bfloat16
I32 = mybir.dt.int32
U32 = mybir.dt.uint32
ALU = mybir.AluOpType
ACT = mybir.ActivationFunctionType
AX = mybir.AxisListType.X

P = 128
NB, SEQ, D = 16, 512, 128
TILES = SEQ // P
NH, DH = 16, 8
FFC = 4
NE, TOPK, GROUPS, TOPG = 32, 4, 8, 4
GE = NE // GROUPS
NTOK = NB * SEQ
CAP = int(1.25 * NTOK * TOPK / NE)
CT = CAP // P
W_AT, ID_AT = D, D + NE
ROW = D + NE + 1
SLOTS = 20
PARTS_Q = (0, 1, 2, 0, 1, 0)
PARTS_K = (0, 0, 0, 1, 1, 2)
NS = len(PARTS_Q)
LN_EPS, SUM_EPS = 1e-5, 1e-9
PE_AT = {"t1": -18, "sf": -15, "t2": -10, "q": -9, "k": -7, "v": -5, "pv": (3, 5, 6, 5), "by_token": 9, "ct": 27, "wo": 29, "t3": 35, "ff1": (36, 37, 37, 38), "ff2": (41, 41, 42, 42), "t4": 48, "logits": 52, "counts": 67}
ACT_AT = {"n1T": -18, "n2T": -10, "q_out": -9, "k_out": -7, "q_part2": -7, "k_part2": -6, "save": 6, "ctT": 28, "n3T": 35, "h1": (36, 37, 37, 38), "x2T": 48, "exp": 55}
DVE_AT = {"stats0": -23, "aggr0": -22, "norm0": -19, "x1": -15, "stats1": -14, "aggr1": -13, "norm1": -11, "v_out": -3, "den": 9, "rden": 10, "ctx": 11, "xm": 29, "stats2": 31, "aggr2": 32, "norm2": 34, "xf": 42, "stats3": 43, "aggr3": 45, "norm3": 47, "lg": 52, "group_max": 53, "group_top": 54, "group_idx": 55, "ex_sum": 56, "rz": 57, "group_eq": 56, "group_left": 57, "masked": 58, "top": 59, "top_idx": 60, "top_eq": 61, "sel": 64, "pos": 68, "weight_sum": 68, "over": 69, "rws": 70, "chosen": 71, "slots8": 72, "idx": 73}
POOL_AT = {"xsf": -23, "rstd0": -22, "rstd1": -12, "x1b": -8, "xfb": -8, "q_less1": -8, "k_less1": -6, "q_less2": -6, "k_less2": -5, "rstd2": 32, "xs": 31, "rstd3": 46, "exs": 54, "sw": 58, "wm": 67, "row": 71, "scatter": (73, 74, 74, 75, 77, 77, 78, 78, 78, 79, 80, 81, 82, 83, 84, 85)}
FAR = 65536.0


class Batch:

    def __init__(self, r, k, copies=2):
        self.r, self.k, self.copies = r, k, copies
        self.n = copies * r + k
        self.par = k % copies
        self.half = r + k // copies

    def shift(self, by):
        return Batch(self.r, self.k + by, self.copies)

    def live(self):
        return not isinstance(self.n, int) or 0 <= self.n < NB


def after(engine, semaphore, value):
    if isinstance(value, int) and value <= 0:
        return
    engine.wait_ge(semaphore, value)


def due(b, slot, at):
    sequence = b.shift(-(at // SLOTS))
    return sequence if at % SLOTS == slot and sequence.live() else None


def done_before(sequence, at, other):
    count = sequence.n - (other - at) // SLOTS
    return min(count, NB) if isinstance(count, int) else count


def run_sequences(engine, iteration):
    for b in range(-2, 6):
        iteration(Batch(0, b))
    with engine.Fori(3, NB // 2 - 1) as r:
        iteration(Batch(r, 0))
        iteration(Batch(r, 1))
    for b in range(NB - 2, NB + 4):
        iteration(Batch(0, b))


def build(nc, x, sfT, maskT, wqT, wkT, wvT, woT, ff1T, ff2T, sf_b, bq, bk, bv, bo, ff1_b, ff2_b,
          g1, b1, g2, b2, g3, b3, wgT, w1, w2, w3, sw1, sw2, sw3, out):
    x_v = x.rearrange("b (t p) d -> b p t d", p=P)
    out_v = out.rearrange("b (t p) d -> b p t d", p=P)
    slots = nc.dram_tensor("slots", [NE * CAP, ROW], FP32, kind="Internal").ap()
    slots_v = slots.rearrange("(e c p) r -> e p c r", p=P, c=CT)
    ysum = [nc.dram_tensor(f"ysum{i}", [NTOK + CAP, D], FP32, kind="Internal").ap() for i in range(2)]
    ysum_v = [y[0:NTOK, :].rearrange("(b t p) d -> b p t d", p=P, t=TILES) for y in ysum]

    z = nc.dram_tensor("z", [NTOK, D], FP32, kind="Internal").ap()
    z_v = z.rearrange("(b t p) d -> b p t d", p=P, t=TILES)
    xT = nc.dram_tensor("xT", [NB, D, SEQ], FP32, kind="Internal").ap()

    with ExitStack() as ctx:
        place = ctx

        def sb(name, shape, dt=FP32):
            return place.enter_context(nc.sbuf_tensor(name, shape, dt))

        def pair(name, shape, dt=FP32):
            return [sb(f"{name}_{i}", shape, dt) for i in range(2)]

        def sem(name):
            return ctx.enter_context(nc.semaphore(name))

        SFT, MASKT, SFW = sb("SFT", [P, D]), sb("MASKT", [P, D]), sb("SFW", [P, D])
        WQ, WK, WV, WO = sb("WQ", [P, D]), sb("WK", [P, D]), sb("WV", [P, D]), sb("WO", [P, D])
        FF1, FF2 = sb("FF1", [P, FFC * P]), sb("FF2", [P, FFC, D])
        WG = sb("WG", [P, NE])
        SW1, SW2, SW3 = sb("SW1", [P, D]), sb("SW2", [P, D]), sb("SW3", [P, D])
        SFB, BV, BO, FF2B = sb("SFB", [P, D]), sb("BV", [P, D]), sb("BO", [P, D]), sb("FF2B", [P, D])
        BQ, BK, BQS = sb("BQ", [P, 1]), sb("BK", [P, 1]), sb("BQS", [P, 1])
        G1, B1, G2, B2 = sb("G1", [P, 1]), sb("B1", [P, 1]), sb("G2", [P, 1]), sb("B2", [P, 1])
        G3, B3, FF1B = sb("G3", [P, 1]), sb("B3", [P, 1]), sb("FF1B", [P, FFC])
        IDENT = sb("IDENT", [P, P])
        CAUSAL = sb("CAUSAL", [P, 2 * P])
        EARLIER, ALLONE = sb("EARLIER", [P, P], BF16), sb("ALLONE", [P, P], BF16)
        NEGHALF, EPS, ZERO, STEP = (sb(n, [P, TILES]) for n in ("NEGHALF", "EPS", "ZERO", "STEP"))
        IOTA_I = sb("IOTA_I", [P, NE], I32)
        IOTA_E, SLOT0 = sb("IOTA_E", [P, NE]), sb("SLOT0", [P, NE])
        TOK_I, TOK = sb("TOK_I", [P, CT], I32), sb("TOK", [P, CT])
        FILL = sb("FILL", [P, CT, ROW])

        TICK, HOLD, POOL_HOLD = sb("TICK", [P, 1]), sb("HOLD", [P, 9]), sb("POOL_HOLD", [P, TILES])
        HOLDS = pair("HOLDS", [P, 1])
        seq_scope = ExitStack()
        place = seq_scope
        X, X1B, XFB = pair("X", [P, TILES, D]), pair("X1B", [P, TILES, D]), pair("XFB", [P, TILES, D])
        X1 = sb("X1", [P, TILES, D])
        XM = sb("XM", [P, TILES, D])
        XS = sb("XS", [P, TILES, D])
        NORM_C, NORM_D = sb("NORM_C", [P, TILES, D]), sb("NORM_D", [P, TILES, D])
        NORM = [NORM_C, NORM_C, NORM_D]
        NORMT_C, NORMT_D = sb("NORMT_C", [P, SEQ]), sb("NORMT_D", [P, SEQ])
        NORMT = [NORMT_C, NORMT_C, NORMT_D]
        STATS = [sb(f"STATS{i}", [P, TILES, 6]) for i in range(4)]
        MV = [sb(f"MV{i}", [P, TILES, 2]) for i in range(4)]
        VE = [sb(f"VE{i}", [P, TILES]) for i in range(4)]
        RSTD = [sb(f"RSTD{i}", [P, TILES]) for i in range(4)]
        QF, KF = sb("QF", [P, SEQ]), sb("KF", [P, SEQ])
        QP = [sb(f"QP{i}", [P, SEQ], BF16) for i in range(3)]
        KP = [sb(f"KP{i}", [P, SEQ], BF16) for i in range(3)]
        QS, KS = pair("QS", [P, NH, SEQ], BF16), pair("KS", [P, NH, SEQ], BF16)
        VONE = pair("VONE", [P, TILES, NH, DH + 1])
        ATT = pair("ATT", [P, 5, 2, 512])
        OSB = sb("OSB", [P, SEQ])
        DEN, RDEN = sb("DEN", [P, TILES, 4]), sb("RDEN", [P, TILES, 4])
        CTX, CTXT = sb("CTX", [P, TILES, D]), sb("CTXT", [P, SEQ])
        H1 = sb("H1", [P, FFC, SEQ])
        ROWS = pair("ROWS", [P, TILES, ROW])
        X2T = sb("X2T", [P, SEQ])
        LG, ML = sb("LG", [P, TILES, NE]), sb("ML", [P, TILES, NE])
        GM, GM8 = sb("GM", [P, TILES, GROUPS]), sb("GM8", [P, TILES, 8])
        GI, IX = sb("GI", [P, TILES, 8], U32), sb("IX", [P, TILES, 8], U32)
        RMAX, ZSUM, RZ = sb("RMAX", [P, TILES]), sb("ZSUM", [P, TILES]), sb("RZ", [P, TILES])
        NEG, LEFT = sb("NEG", [P, TILES * GROUPS, TOPG]), sb("LEFT", [P, TILES * GROUPS])
        M8 = sb("M8", [P, TILES, 8])
        EQE = sb("EQE", [P, TILES, NE, TOPK])
        SEL = sb("SEL", [P, TILES + 1, NE], BF16)
        EXS, EX, SW, WM = (sb(n, [P, TILES, NE]) for n in ("EXS", "EX", "SW", "WM"))
        WS, WSE, RWS = sb("WS", [P, TILES]), sb("WSE", [P, TILES]), sb("RWS", [P, TILES])
        POS, PB, OVER, PO, PV = (sb(n, [P, TILES, NE]) for n in ("POS", "PB", "OVER", "PO", "PV"))
        CARRY, TOTAL = sb("CARRY", [P, NE]), sb("TOTAL", [P, NE])
        D8 = sb("D8", [P, TILES, 8])
        IDX = pair("IDX", [P, TILES, TOPK], I32)

        SC = ctx.enter_context(nc.psum_tensor("SC", [P, 4, 512], FP32))
        O = ctx.enter_context(nc.psum_tensor("O", [P, 512], FP32))
        LA = ctx.enter_context(nc.psum_tensor("LA", [P, 512], FP32))
        LB = ctx.enter_context(nc.psum_tensor("LB", [P, 512], FP32))
        LC = ctx.enter_context(nc.psum_tensor("LC", [P, 512], FP32))

        const_in, filled = sem("const_in"), sem("filled")
        x_in = [sem("x_in0"), sem("x_in1")]
        stack_in = [sem("stack_in0"), sem("stack_in1")]
        rows_sent = [sem("rows_sent0"), sem("rows_sent1")]
        y_stored = [sem("y_stored0"), sem("y_stored1")]
        xT_saved = sem("xT_saved")
        tok_next = sem("tok_next")
        setup_pool, setup_dve, setup_act = sem("setup_pool"), sem("setup_dve"), sem("setup_act")
        second_zeroed = sem("second_zeroed")
        dve_slots = sem("dve_slots")
        (xsf_ready, n1_ready, t1_done, n1T_ready, sf_done, x1_ready, x_used, n2_ready, t2_done,
         n2T_ready, q_done, q01_ready, qr_ready, q2_ready, q3_ready, k_done, k01_ready, kr_ready, k2_ready,
         k3_ready, v_done, v_ready) = (sem(n) for n in (
            "xsf_ready", "n1_ready", "t1_done", "n1T_ready", "sf_done", "x1_ready", "x_used",
            "n2_ready", "t2_done", "n2T_ready", "q_done", "q01_ready", "qr_ready", "q2_ready", "q3_ready",
            "k_done", "k01_ready", "kr_ready", "k2_ready", "k3_ready", "v_done", "v_ready"))
        aggr_done = [sem(f"aggr_done{i}") for i in range(4)]
        eps_added = [sem(f"eps_added{i}") for i in range(4)]
        rstd_ready = [sem(f"rstd_ready{i}") for i in range(4)]
        sc_ready, relu_act, relu_dve = sem("sc_ready"), sem("relu_act"), sem("relu_dve")
        pv_done, o_saved, ot_done, ctx_ready = sem("pv_done"), sem("o_saved"), sem("ot_done"), sem("ctx_ready")
        (ct_done, ctT_ready, wo_done, xm_ready, xs_ready, n3_ready, t3_done, n3T_ready, ff2_done,
         xf_ready) = (sem(n) for n in ("ct_done", "ctT_ready", "wo_done", "xm_ready", "xs_ready", "n3_ready",
                                       "t3_done", "n3T_ready", "ff2_done", "xf_ready"))
        ff1_done, h1_ready = sem("ff1_done"), sem("h1_ready")
        (x2_ready, t4_done, x2T_ready, logits_done, lg_ready, rmax_ready, exs_ready, ex_ready, rz_ready,
         sw_ready, sel_ready, wm_ready, counts_done, pos_ready, carry_ready, rws_ready, row_ready,
         idx_ready) = (sem(n) for n in (
            "x2_ready", "t4_done", "x2T_ready", "logits_done", "lg_ready", "rmax_ready", "exs_ready", "ex_ready",
            "rz_ready", "sw_ready", "sel_ready", "wm_ready", "counts_done", "pos_ready", "carry_ready",
            "rws_ready", "row_ready", "idx_ready"))

        consts = [(SFT[:, :], sfT), (MASKT[:, :], maskT), (WQ[:, :], wqT), (WK[:, :], wkT), (WV[:, :], wvT),
                  (WO[:, :], woT), (FF1[:, :], ff1T), (FF2[:, :, :], ff2T.rearrange("(c f) d -> f c d", f=P)),
                  (WG[:, :], wgT), (SW1[:, :], sw1), (SW2[:, :], sw2), (SW3[:, :], sw3),
                  (SFB[:, :], sf_b.partition_broadcast(P)), (BV[:, :], bv.partition_broadcast(P)),
                  (BO[:, :], bo.partition_broadcast(P)), (FF2B[:, :], ff2_b.partition_broadcast(P)),
                  (BQ[:, :], bq), (BK[:, :], bk), (G1[:, :], g1), (B1[:, :], b1), (G2[:, :], g2),
                  (B2[:, :], b2), (G3[:, :], g3), (B3[:, :], b3), (FF1B[:, :], ff1_b)]
        CONST_IN = 16 * len(consts)
        SETUP_POOL, SETUP_DVE = 16, 10
        WHOLE = NTOK // CAP
        FILLS = NE + WHOLE + 3
        STACKED = 16 * 2 * NS
        SENT = 16 * TILES * TOPK
        seq_block = seq_scope.enter_context(nc.Block())

        @seq_block.sync
        def _(sp):
            sp.dma_start(X[0][:, :, :], x_v[0]).then_inc(x_in[0], 16)
            for dst, src in consts[0::2]:
                sp.dma_start(dst, src).then_inc(const_in, 16)

            def iteration(b):
                c, e, nxt = b.shift(1), b.shift(-2), b.shift(2)
                if nxt.live() and not (isinstance(nxt.n, int) and nxt.n == 0):
                    after(sp, x_used, nxt.n - 1)
                    sp.dma_start(X[nxt.par][:, :, :], x_v[bass.ds(nxt.n, 1)].rearrange("o p t d -> (o p) t d")
                                 ).then_inc(x_in[nxt.par], 16)
                if e.live():
                    sp.wait_ge(x2_ready, e.n + 1)
                    sp.dma_start(ysum_v[0][bass.ds(e.n, 1)].rearrange("o p t d -> (o p) t d"),
                                 ROWS[e.par][:, :, 0:D]).then_inc(y_stored[e.par], 16)
                    sp.wait_ge(x2T_ready, e.n + 1)
                    sp.dma_start(xT[bass.ds(e.n, 1)].rearrange("o d t -> (o d) t"), X2T[:, :]).then_inc(xT_saved, 16)
                if c.live():
                    after(sp, sc_ready, SLOTS * (c.n - 1))
                    if isinstance(c.n, int) and c.n == 1:
                        sp.wait_ge(second_zeroed, 2)
                    for stack, parts, order, ready in (
                            (QS, QP, PARTS_Q, (q01_ready, q2_ready, q3_ready)),
                            (KS, KP, PARTS_K, (k01_ready, k2_ready, k3_ready))):
                        for part in range(3):
                            sp.wait_ge(ready[part], c.n + 1)
                            for at in range(NS):
                                if order[at] == part:
                                    sp.dma_start(
                                        stack[c.par][DH * at:DH * (at + 1), :, :],
                                        parts[part][:, :].rearrange_multi_partition(
                                            "(d h) t -> d h t", d=DH).to_physical()
                                    ).then_inc(stack_in[c.par], 16)

            run_sequences(sp, iteration)

        @seq_block.gpsimd
        def _(pool):
            nc.gpsimd.memset(IDENT[:, :], 0.0).then_inc(setup_pool, 1)
            nc.gpsimd.memset(CAUSAL[:, :], 1.0).then_inc(setup_pool, 1)
            nc.gpsimd.memset(EARLIER[:, :], 1.0).then_inc(setup_pool, 1)
            nc.gpsimd.memset(NEGHALF[:, :], -0.5).then_inc(setup_pool, 1)
            nc.gpsimd.memset(EPS[:, :], LN_EPS).then_inc(setup_pool, 1)
            nc.gpsimd.memset(ZERO[:, :], 0.0).then_inc(setup_pool, 1)
            nc.gpsimd.memset(STEP[:, :], float(SEQ)).then_inc(setup_pool, 1)
            nc.gpsimd.iota(IOTA_I[:, :], pattern=[[1, NE]], base=0, channel_multiplier=0).then_inc(setup_pool, 1)
            nc.gpsimd.iota(TOK_I[:, :], pattern=[[P, CT]], base=0, channel_multiplier=1).then_inc(setup_pool, 1)
            pool.wait_ge(setup_pool, 9)
            nc.gpsimd.affine_select(out=IDENT[:, :], in_=IDENT[:, :], compare_op=ALU.not_equal, fill=1.0, base=0,
                                    pattern=[[-1, P]], channel_multiplier=1).then_inc(setup_pool, 1)
            causal2 = CAUSAL[:, :].rearrange("p (a q) -> p a q", a=2)
            nc.gpsimd.affine_select(out=causal2, in_=causal2, compare_op=ALU.is_ge, fill=0.0, base=0,
                                    pattern=[[0, 2], [1, P]], channel_multiplier=-1).then_inc(setup_pool, 1)
            nc.gpsimd.affine_select(out=EARLIER[:, :], in_=EARLIER[:, :], compare_op=ALU.is_gt, fill=0.0, base=0,
                                    pattern=[[1, P]], channel_multiplier=-1).then_inc(setup_pool, 1)
            nc.gpsimd.tensor_copy(IOTA_E[:, :], IOTA_I[:, :]).then_inc(setup_pool, 1)
            nc.gpsimd.tensor_copy(TOK[:, :], TOK_I[:, :]).then_inc(setup_pool, 1)
            pool.wait_ge(setup_pool, 14)
            nc.gpsimd.tensor_scalar(SLOT0[:, :], IOTA_E[:, :], float(CAP), 1.0, ALU.mult, ALU.add
                                    ).then_inc(setup_pool, 1)
            nc.gpsimd.memset(KS[0][:, :, :], 0.0).then_inc(setup_pool, 1)
            pool.wait_ge(const_in, CONST_IN)
            last_slot = pool.to_reg(NE * CAP - 1)

            def rstd(i, b):
                pool.wait_ge(aggr_done[i], b.n + 1)
                nc.gpsimd.tensor_tensor(VE[i][:, :], MV[i][:, :, 1], EPS[:, :], ALU.add).then_inc(eps_added[i], 1)
                pool.wait_ge(eps_added[i], b.n + 1)
                nc.gpsimd.tensor_tensor(RSTD[i][:, :], VE[i][:, :], NEGHALF[:, :], ALU.pow
                                        ).then_inc(rstd_ready[i], 1)

            def row_bc(vec):
                return vec[:, :].unsqueeze(1).to_broadcast([P, TILES, D])

            def scatter(f, at):
                tile, k = divmod(at, TOPK)
                if at == 0:
                    pool.wait_ge(idx_ready, f.n + 1)
                    pool.wait_ge(row_ready, 2 * (f.n + 1))
                    nc.gpsimd.tensor_tensor(TOK[:, 0:TILES], TOK[:, 0:TILES], STEP[:, :], ALU.add
                                            ).then_inc(tok_next, 1)
                    if isinstance(f.n, int) and f.n == 0:
                        pool.wait_ge(filled, 16 * FILLS)
                pool.indirect_dma_start(
                    out=slots[:, :], out_offset=bass.IndirectOffsetOnAxis(ap=IDX[f.par][:, tile, k:k + 1], axis=0),
                    in_=ROWS[f.par][:, tile, :], in_offset=None, bounds_check=last_slot, oob_is_err=False,
                ).then_inc(rows_sent[f.par], 16)

            def iteration(b):
                for s in range(SLOTS):
                    if isinstance(b.n, int) and b.n == -1 and s in (4, 14):
                        nc.gpsimd.memset((QS, KS)[s == 14][1][:, :, :], 0.0).then_inc(second_zeroed, 1)
                    if c := due(b, s, POOL_AT["xsf"]):
                        pool.wait_ge(x_in[c.par], 16 * (c.half + 1))
                        after(pool, x_used, c.n)
                        nc.gpsimd.tensor_tensor(X1[:, :, :], X[c.par][:, :, :], row_bc(SFB), ALU.add
                                                ).then_inc(xsf_ready, 1)
                    if c := due(b, s, POOL_AT["rstd0"]):
                        rstd(0, c)
                    if c := due(b, s, POOL_AT["rstd1"]):
                        rstd(1, c)
                    if c := due(b, s, POOL_AT["x1b"]):
                        pool.wait_ge(x1_ready, c.n + 1)
                        after(pool, xs_ready, c.n - 1)
                        nc.gpsimd.tensor_tensor(X1B[c.par][:, :, :], X1[:, :, :], row_bc(BO), ALU.add)
                    if c := due(b, s, POOL_AT["xfb"]):
                        after(pool, xs_ready, c.n - 1)
                        nc.gpsimd.tensor_tensor(XFB[c.par][:, :, :], X[c.par][:, :, :], row_bc(FF2B), ALU.add
                                                ).then_inc(x_used, 1)
                    if c := due(b, s, POOL_AT["q_less1"]):
                        pool.wait_ge(q01_ready, c.n + 1)
                        nc.gpsimd.tensor_tensor(QF[:, :], QF[:, :], QP[0][:, :], ALU.subtract
                                                ).then_inc(qr_ready, 1)
                    if c := due(b, s, POOL_AT["k_less1"]):
                        pool.wait_ge(k01_ready, c.n + 1)
                        nc.gpsimd.tensor_tensor(KF[:, :], KF[:, :], KP[0][:, :], ALU.subtract
                                                ).then_inc(kr_ready, 1)
                    if c := due(b, s, POOL_AT["q_less2"]):
                        pool.wait_ge(q2_ready, c.n + 1)
                        nc.gpsimd.tensor_tensor(QP[2][:, :], QF[:, :], QP[1][:, :], ALU.subtract
                                                ).then_inc(q3_ready, 1)
                    if c := due(b, s, POOL_AT["k_less2"]):
                        pool.wait_ge(k2_ready, c.n + 1)
                        nc.gpsimd.tensor_tensor(KP[2][:, :], KF[:, :], KP[1][:, :], ALU.subtract
                                                ).then_inc(k3_ready, 1)
                    if d := due(b, s, POOL_AT["rstd2"]):
                        rstd(2, d)
                    if d := due(b, s, POOL_AT["xs"]):
                        pool.wait_ge(xm_ready, d.n + 1)
                        after(pool, x2_ready, d.n)
                        nc.gpsimd.tensor_tensor(XS[:, :, :], XM[:, :, :], XFB[d.par][:, :, :], ALU.add
                                                ).then_inc(xs_ready, 1)
                    if e := due(b, s, POOL_AT["rstd3"]):
                        rstd(3, e)
                    if e := due(b, s, POOL_AT["exs"]):
                        pool.wait_ge(rmax_ready, e.n + 1)
                        nc.gpsimd.tensor_tensor(EXS[:, :, :], LG[:, :, :],
                                                RMAX[:, :].unsqueeze(2).to_broadcast([P, TILES, NE]),
                                                ALU.subtract).then_inc(exs_ready, 1)
                    if e := due(b, s, POOL_AT["sw"]):
                        pool.wait_ge(rz_ready, e.n + 1)
                        nc.gpsimd.tensor_tensor(SW[:, :, :], EX[:, :, :],
                                                RZ[:, :].unsqueeze(2).to_broadcast([P, TILES, NE]),
                                                ALU.mult).then_inc(sw_ready, 1)
                    if e := due(b, s, POOL_AT["wm"]):
                        pool.wait_ge(sel_ready, e.n + 1)
                        pool.wait_ge(sw_ready, e.n + 1)
                        nc.gpsimd.tensor_tensor(WM[:, :, :], SW[:, :, :], SEL[:, 0:TILES, :], ALU.mult
                                                ).then_inc(wm_ready, 1)
                    if f := due(b, s, POOL_AT["row"]):
                        pool.wait_ge(rws_ready, f.n + 1)
                        nc.gpsimd.tensor_tensor(ROWS[f.par][:, :, W_AT:W_AT + NE], WM[:, :, :],
                                                RWS[:, :].unsqueeze(2).to_broadcast([P, TILES, NE]),
                                                ALU.mult).then_inc(row_ready, 1)
                        after(pool, tok_next, f.n)
                        nc.gpsimd.tensor_tensor(ROWS[f.par][:, :, ID_AT], TOK[:, 0:TILES], ZERO[:, :], ALU.add
                                                ).then_inc(row_ready, 1)
                    for at in range(TILES * TOPK):
                        if f := due(b, s, POOL_AT["scatter"][at]):
                            scatter(f, at)

            run_sequences(pool, iteration)

        @seq_block.vector
        def _(dve):
            ticks = [0]

            def base(b):
                return (b.n + 2) * SLOTS

            nc.vector.memset(FILL[:, :, :], 0.0).then_inc(setup_dve, 1)
            nc.vector.memset(ALLONE[:, :], 1.0).then_inc(setup_dve, 1)
            nc.vector.memset(SEL[:, :, :], 0.0).then_inc(setup_dve, 1)
            nc.vector.memset(CARRY[:, :], 0.0).then_inc(setup_dve, 1)
            nc.vector.memset(O[:, :], 0.0).then_inc(setup_dve, 1)
            nc.vector.memset(QS[0][:, :, :], 0.0).then_inc(setup_dve, 1)
            dve.wait_ge(setup_pool, SETUP_POOL)
            for i in range(2):
                nc.vector.memset(VONE[i][:, :, :, DH:DH + 1], 1.0).then_inc(setup_dve, 1)
            dve.wait_ge(setup_dve, 1)
            nc.vector.tensor_scalar(FILL[:, :, ID_AT], TOK[:, :], float(NTOK), None, ALU.add).then_inc(setup_dve, 1)
            dve.wait_ge(const_in, CONST_IN)
            nc.vector.tensor_tensor(SFW[:, :], SFT[:, :], MASKT[:, :], ALU.mult).then_inc(setup_dve, 1)

            def hold(place):
                nc.vector.memset(HOLD[:, place:place + 1], 0.0)

            def stats(i, src):
                for t in range(TILES):
                    last = nc.vector.bn_stats(STATS[i][:, t, :], src[:, t, :])
                return last

            def aggregate(i):
                hold(i)
                for t in range(TILES):
                    last = nc.vector.bn_aggr(MV[i][:, t, :], STATS[i][:, t, :])
                last.then_inc(aggr_done[i], 1)

            def normalise(i, dst, src, b):
                dve.wait_ge(rstd_ready[i], b.n + 1)
                for t in range(TILES):
                    last = nc.vector.tensor_scalar(dst[:, t, 0:D], src[:, t, :], MV[i][:, t, 0:1],
                                                   RSTD[i][:, t:t + 1], ALU.subtract, ALU.mult)
                return last

            def tiles(psum):
                return psum[:, :].rearrange("p (t d) -> p t d", t=TILES)

            def mask_group(b, s):
                hg, j = divmod(s, 5)
                dve.wait_ge(sc_ready, SLOTS * b.n + s + 1)
                if j == 0:
                    after(dve, pv_done, 4 * b.n + hg - 1)
                src = SC[:, 2 * (s % 2):2 * (s % 2) + 2, :]
                dst = ATT[hg % 2][:, j, :, :]
                if j < 2:
                    src, dst, mask = src[:, :, 0:P], dst[:, :, 0:P], CAUSAL[:, 0:P].unsqueeze(1).to_broadcast([P, 2, P])
                elif j < 4:
                    src, dst = src[:, :, 0:2 * P], dst[:, :, 0:2 * P]
                    mask = CAUSAL[:, :].unsqueeze(1).to_broadcast([P, 2, 2 * P])
                else:
                    src = src.rearrange("p a (h q) -> p (a h) q", h=2)[:, :, 0:P]
                    dst = dst.rearrange("p a (h q) -> p (a h) q", h=2)[:, :, 0:P]
                    mask = CAUSAL[:, 0:P].unsqueeze(1).to_broadcast([P, 4, P])
                nc.vector.scalar_tensor_tensor(out=dst, in0=src, scalar=0.0, in1=mask, op0=ALU.max, op1=ALU.mult
                                               ).then_inc(relu_dve, 1)

            def context(b, hg, step):
                lc = LC[:, :].rearrange("p (t h r) -> p t h r", t=TILES, h=4)
                if step == 0:
                    dve.wait_ge(ot_done, 4 * b.n + hg + 1)
                    return nc.vector.tensor_scalar(DEN[:, :, :], lc[:, :, :, DH], SUM_EPS, None, ALU.add)
                if step == 1:
                    return nc.vector.reciprocal(RDEN[:, :, :], DEN[:, :, :])
                dst = CTX[:, :, 4 * DH * hg:4 * DH * (hg + 1)].rearrange("p t (h c) -> p t h c", h=4)
                if hg == 0:
                    after(dve, ct_done, b.n)
                nc.vector.tensor_tensor(dst, lc[:, :, :, 0:DH],
                                        RDEN[:, :, :].unsqueeze(3).to_broadcast([P, TILES, 4, DH]),
                                        ALU.mult).then_inc(ctx_ready, 1)
                return None

            def iteration(b):
                for s in range(SLOTS):
                    if b.live():
                        mask_group(b, s)
                    after(dve, dve_slots, base(b) + s)
                    last = None
                    if c := due(b, s, DVE_AT["stats0"]):
                        dve.wait_ge(x_in[c.par], 16 * (c.half + 1))
                        last = stats(0, X[c.par])
                    if c := due(b, s, DVE_AT["norm0"]):
                        after(dve, t2_done, c.n)
                        normalise(0, NORM[0], X[c.par], c).then_inc(n1_ready, 1)
                        last = None
                    if c := due(b, s, DVE_AT["x1"]):
                        dve.wait_ge(sf_done, c.n + 1)
                        dve.wait_ge(xsf_ready, c.n + 1)
                        nc.vector.tensor_tensor(X1[:, :, :], tiles(LA), X1[:, :, :], ALU.add
                                                       ).then_inc(x1_ready, 1)
                        last = None
                    if c := due(b, s, DVE_AT["stats1"]):
                        last = stats(1, X1)
                    if c := due(b, s, DVE_AT["norm1"]):
                        dve.wait_ge(t1_done, c.n + 1)
                        normalise(1, NORM[1], X1, c).then_inc(n2_ready, 1)
                        last = None
                    if c := due(b, s, DVE_AT["v_out"]):
                        dve.wait_ge(v_done, c.n + 1)
                        after(dve, pv_done, 4 * (c.n - 1))
                        nc.vector.tensor_tensor(
                            VONE[c.par][:, :, :, 0:DH], LA[:, :].rearrange("p (t h c) -> p t h c", t=TILES, h=NH),
                            BV[:, :].rearrange("p (h c) -> p h c", h=NH).unsqueeze(1).to_broadcast(
                                [P, TILES, NH, DH]), ALU.add).then_inc(v_ready, 1)
                        last = None
                    for step, name in enumerate(("den", "rden", "ctx")):
                        for hg in range(4):
                            if q := due(b, s, DVE_AT[name] + 5 * hg):
                                last = context(q, hg, step)
                    if d := due(b, s, DVE_AT["xm"]):
                        dve.wait_ge(wo_done, d.n + 1)
                        dve.wait_ge(x_used, d.n + 1)
                        after(dve, xs_ready, d.n)
                        nc.vector.tensor_tensor(XM[:, :, :], tiles(LB), X1B[d.par][:, :, :], ALU.add
                                                       ).then_inc(xm_ready, 1)
                        last = None
                    if d := due(b, s, DVE_AT["stats2"]):
                        last = stats(2, XM)
                    if d := due(b, s, DVE_AT["norm2"]):
                        after(dve, t3_done, d.n)
                        normalise(2, NORM[2], XM, d).then_inc(n3_ready, 1)
                        last = None
                    if d := due(b, s, DVE_AT["xf"]):
                        dve.wait_ge(ff2_done, d.n + 1)
                        dve.wait_ge(xs_ready, d.n + 1)
                        nc.vector.tensor_tensor(XS[:, :, :], tiles(LB), XS[:, :, :], ALU.add
                                                       ).then_inc(xf_ready, 1)
                        last = None
                    if e := due(b, s, DVE_AT["stats3"]):
                        last = stats(3, XS)
                    if e := due(b, s, DVE_AT["norm3"]):
                        after(dve, rows_sent[e.par], SENT * e.half)
                        after(dve, y_stored[e.par], 16 * e.half)
                        normalise(3, ROWS[e.par], XS, e).then_inc(x2_ready, 1)
                        last = None
                    if e := due(b, s, DVE_AT["lg"]):
                        dve.wait_ge(logits_done, e.n + 1)
                        nc.vector.tensor_copy(LG[:, :, :], LA[:, 0:TILES * NE].rearrange(
                            "p (t e) -> p t e", t=TILES)).then_inc(lg_ready, 1)
                        last = None
                    if e := due(b, s, DVE_AT["group_max"]):
                        nc.vector.tensor_reduce(GM[:, :, :], LG[:, :, :].rearrange(
                            "p t (g m) -> p (t g) m", g=GROUPS), AX, ALU.max)
                        after(dve, exs_ready, e.n)
                        nc.vector.tensor_reduce(RMAX[:, :], LG[:, :, :], AX, ALU.max
                                                       ).then_inc(rmax_ready, 1)
                        last = None
                    if e := due(b, s, DVE_AT["group_top"]):
                        hold(4)
                        for t in range(TILES):
                            last = nc.vector.max(GM8[:, t, :], GM[:, t, :])
                    if e := due(b, s, DVE_AT["group_idx"]):
                        hold(5)
                        for t in range(TILES):
                            last = nc.vector.max_index(GI[:, t, :], GM8[:, t, :], GM[:, t, :])
                    if e := due(b, s, DVE_AT["ex_sum"]):
                        dve.wait_ge(ex_ready, e.n + 1)
                        last = nc.vector.tensor_reduce(ZSUM[:, :], EX[:, :, :], AX, ALU.add)
                    if e := due(b, s, DVE_AT["group_eq"]):
                        last = nc.vector.tensor_tensor(
                            NEG[:, :, :].rearrange("p (t g) m -> p t g m", t=TILES),
                            GI[:, :, 0:TOPG].unsqueeze(2).to_broadcast([P, TILES, GROUPS, TOPG]),
                            IOTA_E[:, 0:GROUPS].unsqueeze(1).unsqueeze(3).to_broadcast([P, TILES, GROUPS, TOPG]),
                            ALU.not_equal)
                    if e := due(b, s, DVE_AT["rz"]):
                        after(dve, sw_ready, e.n)
                        nc.vector.reciprocal(RZ[:, :], ZSUM[:, :]).then_inc(rz_ready, 1)
                        last = None
                    if e := due(b, s, DVE_AT["group_left"]):
                        last = nc.vector.tensor_reduce(LEFT[:, :], NEG[:, :, :], AX, ALU.min)
                    if e := due(b, s, DVE_AT["masked"]):
                        last = nc.vector.scalar_tensor_tensor(
                            out=ML[:, :, :].rearrange("p t (g m) -> p (t g) m", g=GROUPS),
                            in0=LEFT[:, :].unsqueeze(2).to_broadcast([P, TILES * GROUPS, GE]), scalar=-1e30,
                            in1=LG[:, :, :].rearrange("p t (g m) -> p (t g) m", g=GROUPS),
                            op0=ALU.mult, op1=ALU.add)
                    if e := due(b, s, DVE_AT["top"]):
                        hold(6)
                        for t in range(TILES):
                            last = nc.vector.max(M8[:, t, :], ML[:, t, :])
                    if e := due(b, s, DVE_AT["top_idx"]):
                        hold(7)
                        for t in range(TILES):
                            last = nc.vector.max_index(IX[:, t, :], M8[:, t, :], ML[:, t, :])
                    if e := due(b, s, DVE_AT["top_eq"]):
                        for t in range(TILES):
                            last = nc.vector.tensor_tensor(
                                EQE[:, t, :, :],
                                IX[:, t, 0:TOPK].unsqueeze(1).to_broadcast([P, NE, TOPK]),
                                IOTA_E[:, :].unsqueeze(2).to_broadcast([P, NE, TOPK]), ALU.is_equal)
                    if e := due(b, s, DVE_AT["sel"]):
                        after(dve, row_ready, 2 * e.n)
                        after(dve, counts_done, e.n)
                        nc.vector.tensor_reduce(SEL[:, 0:TILES, :], EQE[:, :, :, :], AX, ALU.max
                                                       ).then_inc(sel_ready, 1)
                        last = None
                    if f := due(b, s, DVE_AT["pos"]):
                        dve.wait_ge(counts_done, f.n + 1)
                        nc.vector.tensor_tensor(
                            POS[:, :, :], LA[:, 0:TILES * NE].rearrange("p (t e) -> p t e", t=TILES),
                            CARRY[:, :].unsqueeze(1).to_broadcast([P, TILES, NE]), ALU.add)
                        nc.vector.tensor_copy(TOTAL[:, :], LA[:, TILES * NE:(TILES + 1) * NE]).then_inc(pos_ready, 1)
                        last = None
                    if f := due(b, s, DVE_AT["weight_sum"]):
                        dve.wait_ge(wm_ready, f.n + 1)
                        last = nc.vector.tensor_reduce(WS[:, :], WM[:, :, :], AX, ALU.add)
                    if f := due(b, s, DVE_AT["over"]):
                        nc.vector.tensor_tensor(CARRY[:, :], CARRY[:, :], TOTAL[:, :], ALU.add)
                        nc.vector.tensor_scalar(WSE[:, :], WS[:, :], SUM_EPS, None, ALU.add)
                        nc.vector.tensor_scalar(OVER[:, :, :], POS[:, :, :], float(CAP), FAR, ALU.is_ge, ALU.mult)
                        last = nc.vector.tensor_tensor(PB[:, :, :], POS[:, :, :],
                                                       SLOT0[:, :].unsqueeze(1).to_broadcast([P, TILES, NE]),
                                                       ALU.add)
                    if f := due(b, s, DVE_AT["rws"]):
                        after(dve, row_ready, 2 * f.n)
                        nc.vector.reciprocal(RWS[:, :], WSE[:, :]).then_inc(rws_ready, 1)
                        last = nc.vector.tensor_tensor(PO[:, :, :], PB[:, :, :], OVER[:, :, :], ALU.add)
                    if f := due(b, s, DVE_AT["chosen"]):
                        last = nc.vector.tensor_tensor(PV[:, :, :], PO[:, :, :], SEL[:, 0:TILES, :], ALU.mult)
                    if f := due(b, s, DVE_AT["slots8"]):
                        hold(8)
                        for t in range(TILES):
                            last = nc.vector.max(D8[:, t, :], PV[:, t, :])
                    if f := due(b, s, DVE_AT["idx"]):
                        nc.vector.tensor_scalar(IDX[f.par][:, :, :], D8[:, :, 0:TOPK], 1.0, None,
                                                       ALU.subtract).then_inc(idx_ready, 1)
                        last = None
                    for i in range(4):
                        if q := due(b, s, DVE_AT[f"aggr{i}"]):
                            aggregate(i)
                            last = None
                    if last is None:
                        last = nc.vector.memset(TICK[:, :], 0.0)
                    last.then_inc(dve_slots, 1)

            run_sequences(dve, iteration)

        @seq_block.scalar
        def _(act):
            def rows_of(y, first, last):
                return y[first:last, :].rearrange("(c p) d -> p c d", p=P)

            fills = [(slots_v[i], FILL[:, :, :]) for i in range(NE)]
            fills += [(rows_of(ysum[1], i * CAP, (i + 1) * CAP), FILL[:, :, 0:D]) for i in range(WHOLE)]
            fills += [(rows_of(ysum[1], WHOLE * CAP, NTOK), FILL[:, 0:(NTOK - WHOLE * CAP) // P, 0:D])]
            fills += [(rows_of(y, NTOK, NTOK + CAP), FILL[:, :, 0:D]) for y in ysum]
            assert len(fills) == FILLS
            for dst, src in consts[1::2]:
                act.dma_start(dst, src).then_inc(const_in, 16)
            act.wait_ge(setup_dve, SETUP_DVE - 1)
            act.wait_ge(const_in, CONST_IN)
            nc.scalar.mul(BQS[:, :], BQ[:, :], DH ** -0.5).then_inc(setup_act, 1)

            def relu_group(b, s):
                hg, j = divmod(s, 5)
                act.wait_ge(relu_dve, SLOTS * b.n + s + 1)
                if j == 0:
                    after(act, pv_done, 4 * b.n + hg - 1)
                src = SC[:, 2 * (s % 2):2 * (s % 2) + 2, :]
                dst = ATT[hg % 2][:, j, :, :]
                if j < 4:
                    lo = P if j < 2 else 2 * P
                    src, dst = src[:, :, lo:512], dst[:, :, lo:512]
                else:
                    src = src.rearrange("p a (h q) -> p (a h) q", h=2)[:, :, P:2 * P]
                    dst = dst.rearrange("p a (h q) -> p (a h) q", h=2)[:, :, P:2 * P]
                nc.scalar.activation(dst, src, ACT.Relu).then_inc(relu_act, 1)

            def save_context(b, hg):
                act.wait_ge(pv_done, 4 * b.n + hg + 1)
                after(act, ot_done, 4 * b.n + hg)
                nc.scalar.copy(OSB[:, :], O[:, :]).then_inc(o_saved, 1)

            def iteration(b):
                for s in range(SLOTS):
                    if isinstance(b.n, int) and 2 <= s < 13 and 0 <= 11 * b.n + s - 2 < FILLS:
                        dst, src = fills[11 * b.n + s - 2]
                        act.dma_start(dst, src).then_inc(filled, 16)
                    if b.live():
                        relu_group(b, s)
                    for hg in range(4):
                        if q := due(b, s, ACT_AT["save"] + 5 * hg):
                            save_context(q, hg)
                    if c := due(b, s, ACT_AT["n1T"]):
                        act.wait_ge(t1_done, c.n + 1)
                        after(act, v_done, c.n)
                        nc.scalar.activation(NORMT[0][:, :], LA[:, :], ACT.Identity, bias=B1[:, :],
                                             scale=G1[:, :]).then_inc(n1T_ready, 1)
                    if c := due(b, s, ACT_AT["n2T"]):
                        act.wait_ge(t2_done, c.n + 1)
                        act.wait_ge(sf_done, c.n + 1)
                        nc.scalar.activation(NORMT[1][:, :], LA[:, :], ACT.Identity, bias=B2[:, :],
                                             scale=G2[:, :]).then_inc(n2T_ready, 1)
                    if c := due(b, s, ACT_AT["q_out"]):
                        act.wait_ge(q_done, c.n + 1)
                        after(act, q3_ready, c.n)
                        p = c.shift(-1)
                        if p.live():
                            act.wait_ge(stack_in[p.par], STACKED * (p.half + 1))
                        nc.scalar.activation(QF[:, :], LA[:, :], ACT.Identity, bias=BQS[:, :],
                                             scale=DH ** -0.5)
                        nc.scalar.activation(QP[0][:, :], LA[:, :], ACT.Identity, bias=BQS[:, :],
                                             scale=DH ** -0.5).then_inc(q01_ready, 1)
                    if c := due(b, s, ACT_AT["k_out"]):
                        act.wait_ge(k_done, c.n + 1)
                        after(act, k3_ready, c.n)
                        nc.scalar.activation(KF[:, :], LA[:, :], ACT.Identity, bias=BK[:, :])
                        nc.scalar.activation(KP[0][:, :], LA[:, :], ACT.Identity, bias=BK[:, :]
                                             ).then_inc(k01_ready, 1)
                    if c := due(b, s, ACT_AT["q_part2"]):
                        act.wait_ge(qr_ready, c.n + 1)
                        nc.scalar.copy(QP[1][:, :], QF[:, :]).then_inc(q2_ready, 1)
                    if c := due(b, s, ACT_AT["k_part2"]):
                        act.wait_ge(kr_ready, c.n + 1)
                        nc.scalar.copy(KP[1][:, :], KF[:, :]).then_inc(k2_ready, 1)
                    if d := due(b, s, ACT_AT["ctT"]):
                        act.wait_ge(ct_done, d.n + 1)
                        after(act, wo_done, d.n)
                        nc.scalar.copy(CTXT[:, :], LB[:, :]).then_inc(ctT_ready, 1)
                    if d := due(b, s, ACT_AT["n3T"]):
                        act.wait_ge(t3_done, d.n + 1)
                        after(act, ff1_done, FFC * d.n)
                        nc.scalar.activation(NORMT[2][:, :], LB[:, :], ACT.Identity, bias=B3[:, :],
                                             scale=G3[:, :]).then_inc(n3T_ready, 1)
                    for i in range(FFC):
                        if d := due(b, s, ACT_AT["h1"][i]):
                            act.wait_ge(ff1_done, FFC * d.n + i + 1)
                            if i == 0:
                                after(act, ff2_done, d.n)
                            nc.scalar.activation(H1[:, i, :], (LB, LC)[i % 2][:, :], ACT.Relu, bias=FF1B[:, i:i + 1]
                                                 ).then_inc(h1_ready, 1)
                    if e := due(b, s, ACT_AT["x2T"]):
                        act.wait_ge(t4_done, e.n + 1)
                        after(act, logits_done, e.n)
                        after(act, xT_saved, 16 * e.n)
                        nc.scalar.copy(X2T[:, :], LC[:, :]).then_inc(x2T_ready, 1)
                    if e := due(b, s, ACT_AT["exp"]):
                        act.wait_ge(exs_ready, e.n + 1)
                        after(act, sw_ready, e.n)
                        nc.scalar.activation(EX[:, :, :], EXS[:, :, :], ACT.Exp).then_inc(ex_ready, 1)

            run_sequences(act, iteration)

        @seq_block.tensor
        def _(pe):
            pe.wait_ge(setup_dve, SETUP_DVE)
            pe.wait_ge(setup_pool, SETUP_POOL)
            pe.wait_ge(const_in, CONST_IN)

            LA_USERS = {"t1": (n1T_ready, 1, 1), "logits": (lg_ready, 1, 1), "sf": (x1_ready, 1, 1),
                        "t2": (n2T_ready, 1, 1), "q": (q01_ready, 1, 1), "k": (k01_ready, 1, 1),
                        "v": (v_ready, 1, 1), "counts": (pos_ready, 1, 1)}
            LB_USERS = {"ct": (ctT_ready, 1, 1), "wo": (xm_ready, 1, 1),
                        "t3": (n3T_ready, 1, 1), "ff2": (xf_ready, 1, 1)}
            LC_USERS = {"t4": (x2T_ready, 1, 1)}
            LC_USERS.update({f"by_token_{hg}": (ctx_ready, 4, hg + 1) for hg in range(4)})
            for i in range(FFC):
                (LB_USERS, LC_USERS)[i % 2][f"ff1_{i}"] = (h1_ready, FFC, i + 1)

            def start_of(user):
                if user.startswith("by_token"):
                    return PE_AT["by_token"] + 5 * int(user[-1])
                at = PE_AT[user.split("_")[0]]
                return at[int(user[-1]) if user.startswith("ff1") else 0] if isinstance(at, tuple) else at

            def bank_read(users, user, sequence):
                start = start_of(user)
                others = sorted((name for name in users if name != user),
                                key=lambda name: (start - start_of(name)) % SLOTS)
                for name in others[:1] if not isinstance(sequence.n, int) else others:
                    semaphore, counts, which = users[name]
                    count = done_before(sequence, start, start_of(name))
                    if not isinstance(count, int) or count > 0:
                        pe.wait_ge(semaphore, counts * (count - 1) + which)

            def transposes(psum, src):
                for t in range(TILES):
                    last = nc.tensor.transpose(psum[:, t * P:(t + 1) * P], src(t), IDENT[:, :])
                return last

            def by_token(psum, srcT, weight, width):
                for t in range(TILES):
                    last = nc.tensor.matmul(psum[:, t * width:(t + 1) * width], srcT[:, t * P:(t + 1) * P],
                                            weight, start=True, stop=True)
                return last

            def scores(b, s):
                hg, j = divmod(s, 5)
                if s == 0:
                    pe.wait_ge(stack_in[b.par], STACKED * (b.half + 1))
                after(pe, relu_act, SLOTS * b.n + s - 1)
                q, k = QS[b.par], KS[b.par]
                bank = 2 * (s % 2)

                def block(head, at, col, key):
                    return nc.tensor.matmul(SC[:, at, col:col + SEQ - key * P], k[:, head, key * P:(key + 1) * P],
                                            q[:, head, key * P:SEQ], start=True, stop=True)

                for i in range(2):
                    head = 4 * hg + 2 * (j % 2) + i
                    if j < 2:
                        last = block(head, bank + i, 0, 0)
                    elif j < 4:
                        block(head, bank + i, 0, 3)
                        last = block(head, bank + i, P, 1)
                    else:
                        block(4 * hg + 2 * i, bank + i, 0, 2)
                        last = block(4 * hg + 2 * i + 1, bank + i, 2 * P, 2)
                last.then_inc(sc_ready, 1)

            def context(b, hg, key):
                pe.wait_ge(relu_act, SLOTS * b.n + 5 * hg + (2, 4, 5, 4)[key])
                if key == 0:
                    pe.wait_ge(v_ready, b.n + 1)
                    after(pe, o_saved, 4 * b.n + hg)
                a = ATT[hg % 2]
                for i in range(4):
                    if key == 0:
                        att = a[:, i // 2, i % 2, :]
                    elif key == 1:
                        att = a[:, 2 + i // 2, i % 2, P:512]
                    elif key == 2:
                        att = a[:, 4, i // 2, 2 * P * (i % 2):2 * P * (i % 2 + 1)]
                    else:
                        att = a[:, 2 + i // 2, i % 2, 0:P]
                    last = nc.tensor.matmul(O[32 * i:32 * i + DH + 1, key * P:SEQ], VONE[b.par][:, key, 4 * hg + i, :],
                                            att, start=key == 0, stop=key == 2)
                if key == 2:
                    last.then_inc(pv_done, 1)

            def context_by_token(b, hg):
                pe.wait_ge(o_saved, 4 * b.n + hg + 1)
                bank_read(LC_USERS, f"by_token_{hg}", b)
                transposes(LC, lambda t: OSB[:, t * P:(t + 1) * P]).then_inc(ot_done, 1)

            def iteration(b):
                for s in range(SLOTS):
                    if b.live():
                        scores(b, s)
                    for key in (0, 1, 3, 2):
                        for hg in range(4):
                            if q := due(b, s, PE_AT["pv"][key] + 5 * hg):
                                context(q, hg, key)
                    for hg in range(4):
                        if q := due(b, s, PE_AT["by_token"] + 5 * hg):
                            context_by_token(q, hg)
                    if c := due(b, s, PE_AT["t1"]):
                        pe.wait_ge(n1_ready, c.n + 1)
                        bank_read(LA_USERS, "t1", c)
                        transposes(LA, lambda t: NORM[0][:, t, :]).then_inc(t1_done, 1)
                    if c := due(b, s, PE_AT["sf"]):
                        pe.wait_ge(n1T_ready, c.n + 1)
                        bank_read(LA_USERS, "sf", c)
                        by_token(LA, NORMT[0], SFW[:, :], D).then_inc(sf_done, 1)
                    if c := due(b, s, PE_AT["t2"]):
                        pe.wait_ge(n2_ready, c.n + 1)
                        bank_read(LA_USERS, "t2", c)
                        transposes(LA, lambda t: NORM[1][:, t, :]).then_inc(t2_done, 1)
                    if c := due(b, s, PE_AT["q"]):
                        pe.wait_ge(n2T_ready, c.n + 1)
                        bank_read(LA_USERS, "q", c)
                        nc.tensor.matmul(LA[:, :], WQ[:, :], NORMT[1][:, :], start=True, stop=True
                                         ).then_inc(q_done, 1)
                    if c := due(b, s, PE_AT["k"]):
                        bank_read(LA_USERS, "k", c)
                        nc.tensor.matmul(LA[:, :], WK[:, :], NORMT[1][:, :], start=True, stop=True
                                         ).then_inc(k_done, 1)
                    if c := due(b, s, PE_AT["v"]):
                        bank_read(LA_USERS, "v", c)
                        by_token(LA, NORMT[1], WV[:, :], D).then_inc(v_done, 1)
                    if d := due(b, s, PE_AT["ct"]):
                        pe.wait_ge(ctx_ready, 4 * (d.n + 1))
                        bank_read(LB_USERS, "ct", d)
                        transposes(LB, lambda t: CTX[:, t, :]).then_inc(ct_done, 1)
                    if d := due(b, s, PE_AT["wo"]):
                        pe.wait_ge(ctT_ready, d.n + 1)
                        bank_read(LB_USERS, "wo", d)
                        by_token(LB, CTXT, WO[:, :], D).then_inc(wo_done, 1)
                    if d := due(b, s, PE_AT["t3"]):
                        pe.wait_ge(n3_ready, d.n + 1)
                        bank_read(LB_USERS, "t3", d)
                        transposes(LB, lambda t: NORM[2][:, t, :]).then_inc(t3_done, 1)
                    for i in range(FFC):
                        if d := due(b, s, PE_AT["ff1"][i]):
                            if i == 0:
                                pe.wait_ge(n3T_ready, d.n + 1)
                            bank_read((LB_USERS, LC_USERS)[i % 2], f"ff1_{i}", d)
                            nc.tensor.matmul((LB, LC)[i % 2][:, :], FF1[:, i * P:(i + 1) * P], NORMT[2][:, :],
                                             start=True, stop=True).then_inc(ff1_done, 1)
                    for t in range(TILES):
                        if d := due(b, s, PE_AT["ff2"][t]):
                            if t == 0:
                                pe.wait_ge(h1_ready, FFC * (d.n + 1))
                                bank_read(LB_USERS, "ff2", d)
                            for i in range(FFC):
                                last = nc.tensor.matmul(LB[:, t * P:(t + 1) * P], H1[:, i, t * P:(t + 1) * P],
                                                        FF2[:, i, :], start=i == 0, stop=i == FFC - 1)
                            if t == TILES - 1:
                                last.then_inc(ff2_done, 1)
                    if e := due(b, s, PE_AT["t4"]):
                        pe.wait_ge(x2_ready, e.n + 1)
                        bank_read(LC_USERS, "t4", e)
                        transposes(LC, lambda t: ROWS[e.par][:, t, 0:D]).then_inc(t4_done, 1)
                    if e := due(b, s, PE_AT["logits"]):
                        pe.wait_ge(x2T_ready, e.n + 1)
                        bank_read(LA_USERS, "logits", e)
                        by_token(LA, X2T, WG[:, :], NE).then_inc(logits_done, 1)
                    if e := due(b, s, PE_AT["counts"]):
                        pe.wait_ge(sel_ready, e.n + 1)
                        bank_read(LA_USERS, "counts", e)
                        nc.tensor.matmul(LA[:, 0:(TILES + 1) * NE], EARLIER[:, :],
                                         SEL[:, :, :].rearrange("p t e -> p (t e)"), start=True, stop=False)
                        for t in range(1, TILES + 1):
                            for before in range(t):
                                last = nc.tensor.matmul(LA[:, t * NE:(t + 1) * NE], ALLONE[:, :],
                                                        SEL[:, before, :], start=False,
                                                        stop=t == TILES and before == t - 1)
                        last.then_inc(counts_done, 1)

            run_sequences(pe, iteration)

        seq_scope.close()

        experts_scope = ExitStack()
        place = experts_scope
        W1, W2, W3 = pair("W1", [P, D]), pair("W2", [P, D]), pair("W3", [P, D])
        LIST = pair("LIST", [P, CT, ROW])
        WCOL = pair("WCOL", [P, CT])
        IDS = pair("IDS", [P, CT], I32)
        XE, SH, HT = pair("XE", [P, SEQ]), pair("SH", [P, SEQ]), pair("HT", [P, SEQ])
        XSH = sb("XSH", [P, SEQ])
        OUTB, ZB = pair("OUTB", [P, CT, D]), sb("ZB", [P, TILES, D])
        list_in = [sem("list_in0"), sem("list_in1")]
        held = sem("held")
        added = [sem("added0"), sem("added1")]
        xsh_in, z_stored, tr_done, xe_ready, h1_done, h_done, silu_done, ht_ready, ffn_done, out_saved, ids_ready = (
            sem(n) for n in ("xsh_in", "z_stored", "tr_done", "xe_ready", "eh1_done", "h_done", "silu_done",
                             "ht_ready", "ffn_done", "out_saved", "ids_ready"))
        PAIRS = NE // 2
        SHARED = 2
        CHUNKS = [(0, 0, 4), (0, 4, 4), (0, 8, 2), (SHARED, 0, 2), (1, 0, 4), (1, 4, 4), (1, 8, 2), (SHARED, 2, 2)]
        NCH = len(CHUNKS)
        OWN = [k for k, ch in enumerate(CHUNKS) if ch[0] != SHARED]
        LISTED, ADDED = 16 * 5, 16 * CT
        T_BANK, H1_BANK = [SC[:, 0, :], SC[:, 1, :]], [SC[:, 2, :], SC[:, 3, :]]
        H3_BANK, OUT_BANK = [LA[:, :], LB[:, :]], [LC[:, :], O[:, :]]
        block = experts_scope.enter_context(nc.Block())

        def run_pairs(engine, pair_of):
            pair_of(0, True, False)
            with engine.Fori(1, PAIRS - 1) as p:
                pair_of(p, False, False)
            pair_of(PAIRS - 1, False, True)

        @block.sync
        def _(sp):
            for i in range(2):
                sp.wait_ge(rows_sent[i], SENT * NB // 2)
                sp.wait_ge(y_stored[i], 16 * NB // 2)
            sp.wait_ge(xT_saved, 16 * NB)

            def store_z(p):
                sp.wait_ge(out_saved, (p + 1) * NCH)
                sp.dma_start(z_v[bass.ds(p, 1)].rearrange("o p t d -> (o p) t d"), ZB[:, :, :]).then_inc(z_stored, 16)

            def pair_of(p, first, last):
                for q in range(2):
                    e = p * 2 + q
                    after(sp, out_saved, (p - 1) * NCH + 4 * q + 3)
                    sp.dma_start(LIST[q][:, :, :], slots_v[bass.ds(e, 1)].rearrange("o p c r -> (o p) c r")
                                 ).then_inc(list_in[q], 16)
                    sp.dma_start(WCOL[q][:, :].unsqueeze(2),
                                 slots_v[bass.ds(e, 1), :, :, bass.ds(e + W_AT, 1)].rearrange(
                                     "o p c r -> (o p) c r"), allow_slow_non_contiguous=True).then_inc(list_in[q], 16)
                    for dst, src in ((W1, w1), (W3, w3), (W2, w2)):
                        sp.dma_start(dst[q][:, :], src[bass.ds(e, 1)].rearrange("o i j -> (o i) j")
                                     ).then_inc(list_in[q], 16)
                if not first:
                    store_z(p - 1)
                sp.dma_start(XSH[:, :], xT[bass.ds(p, 1)].rearrange("o d t -> (o d) t")).then_inc(xsh_in, 16)
                if last:
                    store_z(p)

            run_pairs(sp, pair_of)

        @block.gpsimd
        def _(pool):
            def pair_of(p, first, last):
                for q in range(2):
                    pool.wait_ge(ids_ready, p * 2 + q + 1)
                    if not first:
                        pool.wait_ge(added[q], p * ADDED)
                    for k, (who, tile0, n) in enumerate(CHUNKS):
                        if who != q:
                            continue
                        if k % 4 < 2:
                            pool.wait_ge(out_saved, p * NCH + k + 1 + k % 4)
                            after(pool, held, p * 4 + q * 2 + k % 4)
                            nc.gpsimd.tensor_tensor(POOL_HOLD[:, :], ZERO[:, :], ZERO[:, :], ALU.add).then_inc(held, 1)
                        for tile in range(tile0, tile0 + n):
                            pool.indirect_dma_start(
                                out=ysum[q][:, :],
                                out_offset=bass.IndirectOffsetOnAxis(ap=IDS[q][:, tile:tile + 1], axis=0),
                                in_=OUTB[q][:, tile, :], in_offset=None, compute_op=ALU.add,
                            ).then_inc(added[q], 16)

            run_pairs(pool, pair_of)

        @block.scalar
        def _(act):
            def evacuate(p, j):
                act.wait_ge(tr_done, p * len(OWN) + j + 1)
                n = CHUNKS[OWN[j]][2] * P
                back = (p * NCH + OWN[j - 2] + 1) if j >= 2 else (p - 1) * NCH + OWN[j - 2] + 1
                after(act, h_done, back)
                nc.scalar.copy(XE[j % 2][:, 0:n], T_BANK[j % 2][:, 0:n]).then_inc(xe_ready, 1)

            def pair_of(p, first, last):
                if first:
                    evacuate(p, 0)
                for k, (who, tile0, n) in enumerate(CHUNKS):
                    nxt = (k + 1) % NCH
                    if nxt in OWN and not (last and nxt == 0):
                        evacuate(p + (nxt == 0), OWN.index(nxt))
                    act.wait_ge(h_done, p * NCH + k + 1)
                    after(act, ht_ready, p * NCH + k - 1)
                    nc.scalar.activation(SH[k % 2][:, 0:n * P], H1_BANK[k % 2][:, 0:n * P], ACT.Silu
                                         ).then_inc(silu_done, 1)

            run_pairs(act, pair_of)

        @block.vector
        def _(dve):
            def save(p, k):
                who, tile0, n = CHUNKS[k]
                dve.wait_ge(ffn_done, p * NCH + k + 1)
                src = OUT_BANK[k % 2][:, 0:n * P].rearrange("p (t d) -> p t d", d=D)
                if who == SHARED:
                    if tile0 == 0:
                        after(dve, z_stored, p * 16)
                    nc.vector.tensor_copy(ZB[:, tile0:tile0 + n, :], src).then_inc(out_saved, 1)
                else:
                    if tile0 == 0:
                        after(dve, added[who], p * ADDED)
                    nc.vector.tensor_tensor(
                        OUTB[who][:, tile0:tile0 + n, :], src,
                        WCOL[who][:, tile0:tile0 + n].unsqueeze(2).to_broadcast([P, n, D]), ALU.mult
                    ).then_inc(out_saved, 1)

            def pair_of(p, first, last):
                for k, (who, tile0, n) in enumerate(CHUNKS):
                    if who != SHARED and tile0 == 0:
                        dve.wait_ge(list_in[who], (p + 1) * LISTED)
                        after(dve, added[who], p * ADDED)
                        nc.vector.tensor_copy(IDS[who][:, :], LIST[who][:, :, ID_AT]).then_inc(ids_ready, 1)
                    dve.wait_ge(silu_done, p * NCH + k + 1)
                    after(dve, ffn_done, p * NCH + k - 1)
                    nc.vector.tensor_tensor(HT[k % 2][:, 0:n * P], SH[k % 2][:, 0:n * P],
                                            H3_BANK[k % 2][:, 0:n * P], ALU.mult).then_inc(ht_ready, 1)
                    if k > 0:
                        save(p, k - 1)
                    elif not first:
                        save(p - 1, NCH - 1)
                if last:
                    save(p, NCH - 1)

            run_pairs(dve, pair_of)

        @block.tensor
        def _(pe):
            def transpose(p, j):
                who, tile0, n = CHUNKS[OWN[j]]
                if tile0 == 0:
                    pe.wait_ge(list_in[who], (p + 1) * LISTED)
                after(pe, xe_ready, p * len(OWN) + j - 1)
                for t in range(n):
                    last = nc.tensor.transpose(T_BANK[j % 2][:, t * P:(t + 1) * P], LIST[who][:, tile0 + t, 0:D],
                                               IDENT[:, :])
                last.then_inc(tr_done, 1)

            def up(p, k):
                who, tile0, n = CHUNKS[k]
                if who == SHARED:
                    pe.wait_ge(xsh_in, (p + 1) * 16)
                    moving, first_w, third_w = XSH[:, tile0 * P:(tile0 + n) * P], SW1, SW3
                else:
                    j = OWN.index(k)
                    pe.wait_ge(xe_ready, p * len(OWN) + j + 1)
                    moving, first_w, third_w = XE[j % 2][:, 0:n * P], W1[who], W3[who]
                after(pe, ht_ready, p * NCH + k - 1)
                nc.tensor.matmul(H1_BANK[k % 2][:, 0:n * P], first_w[:, :], moving, start=True, stop=True)
                nc.tensor.matmul(H3_BANK[k % 2][:, 0:n * P], third_w[:, :], moving, start=True, stop=True
                                 ).then_inc(h_done, 1)

            def down(p, k):
                who, tile0, n = CHUNKS[k]
                pe.wait_ge(ht_ready, p * NCH + k + 1)
                after(pe, out_saved, p * NCH + k - 1)
                for t in range(n):
                    last = nc.tensor.matmul(OUT_BANK[k % 2][:, t * P:(t + 1) * P], HT[k % 2][:, t * P:(t + 1) * P],
                                            (SW2 if who == SHARED else W2[who])[:, :], start=True, stop=True)
                last.then_inc(ffn_done, 1)

            def pair_of(p, first, last):
                if first:
                    transpose(p, 0)
                for k in range(NCH):
                    nxt = (k + 1) % NCH
                    if nxt in OWN and not (last and nxt == 0):
                        transpose(p + (nxt == 0), OWN.index(nxt))
                    up(p, k)
                    if k > 0:
                        down(p, k - 1)
                    elif not first:
                        down(p - 1, NCH - 1)
                if last:
                    down(p, NCH - 1)

            run_pairs(pe, pair_of)

        experts_scope.close()

        final_scope = ExitStack()
        place = final_scope
        DEPTH = 8
        Y0, Y1, Z, RES = ([sb(f"{name}_{i}", [P, TILES, D]) for i in range(DEPTH)] for name in ("Y0", "Y1", "Z", "RES"))
        FSTATS, FMV = ([sb(f"{name}_{i}", [P, TILES, width]) for i in range(DEPTH)]
                       for name, width in (("FSTATS", 6), ("FMV", 2)))
        FVE, FRSTD = ([sb(f"{name}_{i}", [P, TILES]) for i in range(DEPTH)] for name in ("FVE", "FRSTD"))
        y_in = [sem(f"y_in{i}") for i in range(DEPTH)]
        out_stored = [sem(f"out_stored{i}") for i in range(DEPTH)]
        part_ready, sum_ready, fstats_done, faggr_done, feps_added, frstd_ready, res_ready = (sem(n) for n in (
            "part_ready", "sum_ready", "fstats_done", "faggr_done", "feps_added", "frstd_ready", "res_ready"))
        block = final_scope.enter_context(nc.Block())

        def run_last(engine, step, lag):
            for b in range(DEPTH):
                step(Batch(0, b, DEPTH))
            with engine.Fori(1, NB // DEPTH) as r:
                for k in range(DEPTH):
                    step(Batch(r, k, DEPTH))
            for b in range(NB, NB + lag):
                step(Batch(0, b, DEPTH))

        @block.sync
        def _(sp):
            for q in range(2):
                sp.wait_ge(added[q], ADDED * PAIRS)
            sp.wait_ge(z_stored, 16 * PAIRS)

            def load(b):
                after(sp, res_ready, b.n - DEPTH + 1)
                for dst, src in ((Y0, ysum_v[0]), (Y1, ysum_v[1]), (Z, z_v)):
                    sp.dma_start(dst[b.par][:, :, :], src[bass.ds(b.n, 1)].rearrange("o p t d -> (o p) t d")
                                 ).then_inc(y_in[b.par], 16)

            run_last(sp, load, 0)

        @block.gpsimd
        def _(pool):
            def step(b):
                if b.live():
                    pool.wait_ge(part_ready, b.n + 1)
                    nc.gpsimd.tensor_tensor(Y0[b.par][:, :, :], Y0[b.par][:, :, :], Z[b.par][:, :, :], ALU.add
                                            ).then_inc(sum_ready, 1)
                a = b.shift(-2)
                if a.live():
                    pool.wait_ge(faggr_done, a.n + 1)
                    nc.gpsimd.tensor_tensor(FVE[a.par][:, :], FMV[a.par][:, :, 1], EPS[:, :], ALU.add
                                            ).then_inc(feps_added, 1)
                    pool.wait_ge(feps_added, a.n + 1)
                    nc.gpsimd.tensor_tensor(FRSTD[a.par][:, :], FVE[a.par][:, :], NEGHALF[:, :], ALU.pow
                                            ).then_inc(frstd_ready, 1)

            run_last(pool, step, 2)

        @block.vector
        def _(dve):
            def step(b):
                if b.live():
                    dve.wait_ge(y_in[b.par], 48 * (b.half + 1))
                    nc.vector.tensor_tensor(Y0[b.par][:, :, :], Y0[b.par][:, :, :], Y1[b.par][:, :, :], ALU.add
                                            ).then_inc(part_ready, 1)
                a = b.shift(-1)
                if a.live():
                    dve.wait_ge(sum_ready, a.n + 1)
                    for t in range(TILES):
                        last = nc.vector.bn_stats(FSTATS[a.par][:, t, :], Y0[a.par][:, t, :])
                    last.then_inc(fstats_done, 1)
                a = b.shift(-3)
                if a.live():
                    dve.wait_ge(frstd_ready, a.n + 1)
                    after(dve, out_stored[a.par], 16 * a.half)
                    for t in range(TILES):
                        last = nc.vector.tensor_scalar(RES[a.par][:, t, :], Y0[a.par][:, t, :], FMV[a.par][:, t, 0:1],
                                                       FRSTD[a.par][:, t:t + 1], ALU.subtract, ALU.mult)
                    last.then_inc(res_ready, 1)
                a = b.shift(-1)
                if a.live():
                    dve.wait_ge(fstats_done, a.n + 1)
                    after(dve, res_ready, a.n - DEPTH + 1)
                    nc.vector.memset(HOLDS[a.k % 2][:, :], 0.0)
                    for t in range(TILES):
                        last = nc.vector.bn_aggr(FMV[a.par][:, t, :], FSTATS[a.par][:, t, :])
                    last.then_inc(faggr_done, 1)

            run_last(dve, step, 3)

        @block.scalar
        def _(act):
            def store(b):
                act.wait_ge(res_ready, b.n + 1)
                act.dma_start(out_v[bass.ds(b.n, 1)].rearrange("o p t d -> (o p) t d"), RES[b.par][:, :, :]
                              ).then_inc(out_stored[b.par], 16)

            run_last(act, store, 0)
            for stored in out_stored:
                act.wait_ge(stored, 16 * NB // DEPTH)

        final_scope.close()

_INS = ["x", "sfT", "maskT", "wqT", "wkT", "wvT", "woT", "ff1T", "ff2T", "sf_b", "bq", "bk", "bv", "bo", "ff1_b",
        "ff2_b", "g1", "b1", "g2", "b2", "g3", "b3", "wgT", "w1", "w2", "w3", "sw1", "sw2", "sw3"]


def kernel(**inputs):
    import numpy as _np
    import concourse.bacc as _bacc
    from concourse import mybir as _mybir
    from concourse.bass_utils import run_bass_kernel_spmd as _run

    a = {n.split("_", 2)[2]: v for n, v in inputs.items() if n.startswith("L0_attn_")}
    m = {n.split("_", 2)[2]: v for n, v in inputs.items() if n.startswith("L0_ffn_")}

    def by_width(w):
        w = _np.asarray(w)
        return w.reshape(NH, DH, -1).transpose(1, 0, 2).reshape(w.shape[0], -1)

    def col(v):
        return _np.asarray(v).reshape(-1, 1)

    laid = {"x": a["x"], "sfT": a["sf_w"].T, "maskT": a["mask"].T, "wqT": by_width(a["wq"]).T,
            "wkT": by_width(a["wk"]).T, "wvT": a["wv"].T, "woT": a["wo"].T, "ff1T": a["ff1_w"].T,
            "ff2T": a["ff2_w"].T, "sf_b": a["sf_b"], "bq": by_width(a["bq"]), "bk": by_width(a["bk"]),
            "bv": a["bv"], "bo": a["bo"], "ff1_b": a["ff1_b"].reshape(FFC, P).T, "ff2_b": a["ff2_b"],
            "g1": col(a["g1"]), "b1": col(a["b1"]), "g2": col(a["g2"]), "b2": col(a["b2"]),
            "g3": col(a["g3"]), "b3": col(a["b3"]), "wgT": m["wg"].T, "w1": m["w1"], "w2": m["w2"],
            "w3": m["w3"], "sw1": m["sw1"], "sw2": m["sw2"], "sw3": m["sw3"]}

    nc = _bacc.Bacc("TRN2", target_bir_lowering=False, num_devices=1)
    arrays, args = {}, []
    for name in _INS:
        v = _np.ascontiguousarray(laid[name])
        arrays[f"in_{name}_dram"] = v
        args.append(nc.dram_tensor(f"in_{name}_dram", v.shape, _mybir.dt.from_np(v.dtype), kind="ExternalInput").ap())
    args.append(nc.dram_tensor("out_0_dram", (NB, SEQ, D), _mybir.dt.float32, kind="ExternalOutput").ap())
    build(nc, *args)
    r = _run(nc, [arrays], core_ids=[0])
    return r.results[0]["out_0_dram"]
```
